# Optimizing a Trainium2 kernel written in Bass

```python
import numpy as np
import jax
import jax.numpy as jnp

def _softmax(x, axis=-1):
    return jax.nn.softmax(x, axis=axis)

def _gelu(x):
    return jax.nn.gelu(x, approximate=True)

def _silu(x):
    return jax.nn.silu(x)

def _sigmoid(x):
    return jax.nn.sigmoid(x)

def _layernorm(x, axis=-1, eps=1e-05):
    m = jnp.mean(x, axis=axis, keepdims=True)
    v = jnp.var(x, axis=axis, keepdims=True)
    return (x - m) / jnp.sqrt(v + eps)

def _scatter_add(tgt, idx, src, axis=0):
    return tgt.at[idx].add(src)

def _segment_sum(src, seg, n):
    return jax.ops.segment_sum(src, seg, n)
kernel_name = 'mk_prb_d1_jaxref_r4_1d2902'

def setup_inputs(seed: int=0):
    np.random.seed(seed)
    _w = jnp.asarray

    def _L0_attn_setup():
        import jax, jax.numpy as jnp
        import numpy as np
        import math
        H = 512
        NH = 16
        HD = H // NH
        THETA = 10000.0

        def rotate_half(x):
            x1, x2 = (x[..., :HD // 2], x[..., HD // 2:])
            return jnp.concatenate((-x2, x1), axis=-1)

        def rope_tables(seq_len, dtype):
            inv_freq = 1.0 / THETA ** (np.arange(0, HD, 2, dtype=np.float32) / HD)
            t = np.arange(seq_len, dtype=np.float32)
            freqs = np.einsum('i,j->ij', t, inv_freq)
            emb = np.concatenate((freqs, freqs), axis=-1)
            return (jnp.asarray(np.cos(emb), dtype), jnp.asarray(np.sin(emb), dtype))
        key = jax.random.key(seed)
        ks = jax.random.split(key, 5)
        B, S = (2, 512)
        scale = 1.0 / math.sqrt(H)
        return {'hidden_states': jax.random.normal(ks[0], (B, S, H), jnp.float32), 'Wq': jax.random.normal(ks[1], (H, H), jnp.float32) * scale, 'Wk': jax.random.normal(ks[2], (H, H), jnp.float32) * scale, 'Wv': jax.random.normal(ks[3], (H, H), jnp.float32) * scale, 'Wo': jax.random.normal(ks[4], (H, H), jnp.float32) * scale}
    _L0_attn_in = _L0_attn_setup()

    def _L0_ffn_setup():
        import jax, jax.numpy as jnp
        import numpy as np
        E = 64
        K = 4
        H = 512
        I = 384
        C = 64
        B, S = (1, 512)
        key = jax.random.key(seed)
        ks = jax.random.split(key, 8)
        sh = 1.0 / np.sqrt(H).astype(np.float32)
        si = 1.0 / np.sqrt(I).astype(np.float32)
        return {'x': jax.random.normal(ks[0], (B, S, H), jnp.float32), 'w_router': jax.random.normal(ks[1], (E, H), jnp.float32) * sh, 'w_gate': jax.random.normal(ks[2], (E, H, I), jnp.float32) * sh, 'w_up': jax.random.normal(ks[3], (E, H, I), jnp.float32) * sh, 'w_down': jax.random.normal(ks[4], (E, I, H), jnp.float32) * si, 'w_sh_gate': jax.random.normal(ks[5], (H, I), jnp.float32) * sh, 'w_sh_up': jax.random.normal(ks[6], (H, I), jnp.float32) * sh, 'w_sh_down': jax.random.normal(ks[7], (I, H), jnp.float32) * si}
    _L0_ffn_in = _L0_ffn_setup()
    _d = {'L0_attn_hidden_states': _L0_attn_in['hidden_states'], 'L0_attn_Wq': _L0_attn_in['Wq'], 'L0_attn_Wk': _L0_attn_in['Wk'], 'L0_attn_Wv': _L0_attn_in['Wv'], 'L0_attn_Wo': _L0_attn_in['Wo'], 'L0_ffn_w_router': _L0_ffn_in['w_router'], 'L0_ffn_w_gate': _L0_ffn_in['w_gate'], 'L0_ffn_w_up': _L0_ffn_in['w_up'], 'L0_ffn_w_down': _L0_ffn_in['w_down'], 'L0_ffn_w_sh_gate': _L0_ffn_in['w_sh_gate'], 'L0_ffn_w_sh_up': _L0_ffn_in['w_sh_up'], 'L0_ffn_w_sh_down': _L0_ffn_in['w_sh_down']}
    _x0 = _d['L0_attn_hidden_states']
    _d['L0_attn_hidden_states'] = jax.random.normal(jax.random.fold_in(jax.random.key(seed), 1), (8, 512, 512), dtype=_x0.dtype)
    del _x0
    return _d

def reference(L0_attn_hidden_states, L0_attn_Wq, L0_attn_Wk, L0_attn_Wv, L0_attn_Wo, L0_ffn_w_router, L0_ffn_w_gate, L0_ffn_w_up, L0_ffn_w_down, L0_ffn_w_sh_gate, L0_ffn_w_sh_up, L0_ffn_w_sh_down):

    def _L0_attn_ref(hidden_states, Wq, Wk, Wv, Wo):
        import jax, jax.numpy as jnp
        import numpy as np
        import math
        H = 512
        NH = 16
        HD = H // NH
        THETA = 10000.0

        def rotate_half(x):
            x1, x2 = (x[..., :HD // 2], x[..., HD // 2:])
            return jnp.concatenate((-x2, x1), axis=-1)

        def rope_tables(seq_len, dtype):
            inv_freq = 1.0 / THETA ** (np.arange(0, HD, 2, dtype=np.float32) / HD)
            t = np.arange(seq_len, dtype=np.float32)
            freqs = np.einsum('i,j->ij', t, inv_freq)
            emb = np.concatenate((freqs, freqs), axis=-1)
            return (jnp.asarray(np.cos(emb), dtype), jnp.asarray(np.sin(emb), dtype))
        B, S, _ = hidden_states.shape

        def proj(W):
            y = jnp.einsum('bsh,oh->bso', hidden_states, W)
            return y.reshape(B, S, NH, HD).transpose(0, 2, 1, 3)
        q, k, v = (proj(Wq), proj(Wk), proj(Wv))
        cos, sin = rope_tables(S, hidden_states.dtype)
        cos, sin = (cos[None, None], sin[None, None])
        q = q * cos + rotate_half(q) * sin
        k = k * cos + rotate_half(k) * sin
        scores = jnp.einsum('bhqd,bhkd->bhqk', q, k) / math.sqrt(HD)
        causal = jnp.triu(jnp.ones((S, S), bool), k=1)
        scores = jnp.where(causal, -jnp.inf, scores)
        attn = jax.nn.softmax(scores, axis=-1)
        out = jnp.einsum('bhqk,bhkd->bhqd', attn, v)
        out = out.transpose(0, 2, 1, 3).reshape(B, S, H)
        return jnp.einsum('bsh,oh->bso', out, Wo)

    def _L0_ffn_ref(x, w_router, w_gate, w_up, w_down, w_sh_gate, w_sh_up, w_sh_down):
        import jax, jax.numpy as jnp
        import numpy as np
        E = 64
        K = 4
        H = 512
        I = 384
        C = 64
        B, S = (1, 512)
        b, s, h = x.shape
        xf = x.reshape(-1, h)
        T = xf.shape[0]
        P = T * K
        logits = xf @ w_router.T
        top_vals, top_idx = jax.lax.top_k(logits, K)
        w_tok = jax.nn.softmax(top_vals.astype(jnp.float32), axis=-1)
        e_flat = top_idx.reshape(-1)
        tok_flat = jnp.repeat(jnp.arange(T), K)
        w_flat = w_tok.reshape(-1)
        order = jnp.argsort(e_flat)
        tok_s = tok_flat[order]
        w_s = w_flat[order]
        counts = jnp.zeros((E,), jnp.int32).at[e_flat].add(1)
        offsets = jnp.cumsum(counts) - counts
        pos = offsets[:, None] + jnp.arange(C)[None, :]
        valid = jnp.arange(C)[None, :] < counts[:, None]
        pos_c = jnp.clip(pos, 0, P - 1)
        tok_ec = tok_s[pos_c]
        w_ec = jnp.where(valid, w_s[pos_c], 0.0)
        x_ec = xf[tok_ec]
        g = jax.nn.silu(jnp.einsum('ech,ehi->eci', x_ec, w_gate))
        u = jnp.einsum('ech,ehi->eci', x_ec, w_up)
        y = jnp.einsum('eci,eih->ech', g * u, w_down)
        contrib = (y * w_ec[..., None]).reshape(-1, h)
        combined = jnp.zeros_like(xf).at[tok_ec.reshape(-1)].add(contrib)
        sg = jax.nn.silu(xf @ w_sh_gate)
        su = xf @ w_sh_up
        combined = combined + sg * su @ w_sh_down
        return combined.reshape(b, s, h)
    x = L0_attn_hidden_states
    xn = _layernorm(x, axis=-1)
    x = x + _L0_attn_ref(xn, L0_attn_Wq, L0_attn_Wk, L0_attn_Wv, L0_attn_Wo) + _L0_ffn_ref(xn, L0_ffn_w_router, L0_ffn_w_gate, L0_ffn_w_up, L0_ffn_w_down, L0_ffn_w_sh_gate, L0_ffn_w_sh_up, L0_ffn_w_sh_down)
    return x

_drawn_inputs = setup_inputs


def setup_inputs(seed=0):
    import zlib

    import numpy as np

    out = dict(_drawn_inputs(seed))
    spreads = {}
    factors = {}
    for name, (base, spread) in spreads.items():
        noise = np.random.default_rng([zlib.crc32(name.encode()), seed]).standard_normal(out[name].shape)
        drawn = base * np.exp(spread * noise) if base else spread * noise
        out[name] = jnp.asarray(drawn.astype(out[name].dtype))
    for name, factor in factors.items():
        out[name] = (out[name] * factor).astype(out[name].dtype)
    return out
```

```python
from contextlib import ExitStack

import numpy as np

import concourse.bass as bass
from concourse import mybir

ALU = mybir.AluOpType
ACT = mybir.ActivationFunctionType
AX_X = mybir.AxisListType.X
F32 = mybir.dt.float32
F32R = mybir.dt.float32r
BF16 = mybir.dt.bfloat16
U32 = mybir.dt.uint32

START = 1
FIRST = 16
P = 128
B, S, H = 8, 512, 512
NH, HD = 16, 32
E, TOPK, CAP, I = 64, 4, 64, 384
T = B * S
NT = S // P
KC = H // P
IC = I // P
NG = NH * HD // P
GH = NH // NG
PAIRS = E // 2 // B
assert PAIRS == NG
SCALE = HD ** -0.5
EPS = 1e-5
SPLIT = 3 * HD
SHIFT = SPLIT + 2
KOFF = (0, 512, 1024, 896)
PW = 1280


def split_weights(nc, act, dve, stage, parts, loaded, loads, hi_done, lo_done, n, who):
    src = stage[:, 0:parts[0].shape[1] * parts[0].shape[2]].rearrange("p (a b) -> p a b", b=parts[0].shape[2])
    if who == "act":
        act.wait_ge(loaded, loads)
        nc.scalar.activation(parts[0], src, ACT.Copy).then_inc(hi_done, 1)
    else:
        dve.wait_ge(loaded, loads)
        dve.wait_ge(hi_done, n + 1)
        nc.vector.tensor_tensor(parts[1], src, parts[0].bitcast(F32), ALU.subtract).then_inc(lo_done, 1)


def three_products(nc, out, left, right, chunks):
    last = None
    terms = [(c, a, b) for c in chunks for a, b in ((0, 0), (0, 1), (1, 0))]
    for m, (c, a, b) in enumerate(terms):
        last = nc.tensor.matmul(out, left(a, c), right(b, c), start=(m == 0), stop=(m == len(terms) - 1))
    return last


def build(nc, d):
    with ExitStack() as whole:
        def sbw(name, shape, dt=F32):
            return whole.enter_context(nc.sbuf_tensor(name, shape, dt))

        ident = sbw("ident", [P, P])
        w_parts = [sbw(f"w_{'hl'[a]}", [P, 4, KC, H], F32R) for a in range(2)]
        stage_one(nc, d, ident, w_parts)
        stage_two(nc, d, ident, w_parts)


def stage_one(nc, d, ident, w_parts):
    with ExitStack() as ctx:
        def sb(name, shape, dt=F32):
            return ctx.enter_context(nc.sbuf_tensor(name, shape, dt))

        def sem(name):
            return ctx.enter_context(nc.semaphore(name))

        counts = []

        def count(name):
            counts.append(sem(name))
            return counts[-1]

        def banks(name, n):
            return [ctx.enter_context(nc.psum_tensor(f"{name}{j}", [P, 512], F32)) for j in range(n)]

        tp, gt, up, yb = banks("tp", 2), banks("gt", 2), banks("up", 2), banks("yb", 2)

        stage = sb("stage", [P, KC * H])
        sg = [sb(f"sg_{a}", [P, KC, I], F32R) for a in "hl"]
        su = [sb(f"su_{a}", [P, KC, I], F32R) for a in "hl"]
        sd = [sb(f"sd_{a}", [P, IC, H], F32R) for a in "hl"]
        wr = [sb(f"wr_{a}", [P, KC, P], F32R) for a in "hl"]
        x_in = sb("x_in", [P, 2, NT, H])
        xn = sb("xn", [P, NT, H])
        xT = [sb(f"xT_{a}", [P, KC, S], F32R) for a in "hl"]
        h = sb("h", [P, 2, S])
        hT = [sb(f"hT_{a}", [P, IC, S], F32R) for a in "hl"]
        y_out = sb("y_out", [P, 2, H])
        stat = sb("stat", [P, NT, 6])
        mv = sb("mv", [P, NT, 2])
        veps = sb("veps", [P, NT])
        rstd = sb("rstd", [P, NT])
        neg_half = sb("neg_half", [P, NT])
        idle = sb("idle", [P, 1])
        pool_idle = sb("pool_idle", [P, 1])
        lgT = sb("lgT", [P, S])
        lg = sb("lg", [P, NT, E])
        top = sb("top", [P, NT, 8])
        top_i = sb("top_i", [P, NT, 8], U32)
        ex = sb("ex", [P, NT, TOPK])
        esum = sb("esum", [P, NT])
        wtok = sb("wtok", [P, NT, TOPK])
        idx_f = sb("idx_f", [P, NT * TOPK])
        iota_e = sb("iota_e", [P, E])
        onehot = sb("onehot", [P, NT * TOPK, E])
        prod = sb("prod", [P, NT * TOPK, E])
        chosen = sb("chosen", [P, NT, E], BF16)
        chosen_sum = sb("chosen_sum", [P, E])
        before = sb("before", [P, E])
        before_b = sb("before_b", [P, E], BF16)
        lower = sb("lower", [P, P])
        lower_b = sb("lower_b", [P, P], BF16)
        ones_b = sb("ones_b", [P, P], BF16)
        tok = sb("tok", [P, NT])
        spill = sb("spill", [P, NT * TOPK])
        place = sb("place", [P, NT * TOPK])
        fits = sb("fits", [P, NT * TOPK])
        row = sb("row", [P, NT * TOPK])
        row_u = sb("row_u", [P, 2, NT * TOPK], U32)
        entry = sb("entry", [P, 2, NT * TOPK, 2])

        const_in = sem("const_in")
        init_done = sem("init_done")
        w_loaded = sem("w_loaded")
        w_hi, w_lo = sem("w_hi"), sem("w_lo")
        x_loaded = [count(f"x_loaded{u}") for u in range(2)]
        x_free = [count(f"x_free{u}") for u in range(2)]
        dv = count("dv")
        var_ready, rstd_ready, pool_const = count("var_ready"), count("rstd_ready"), sem("pool_const")
        xn_ready, xn_stored = count("xn_ready"), count("xn_stored")
        tp_full, logits_read, rank_read = count("tp_full"), count("logits_read"), count("rank_read")
        xT_hi, xT_lo = count("xT_hi"), count("xT_lo")
        lgT_ready, ex_in, ex_ready = count("lgT_ready"), count("ex_in"), count("ex_ready")
        gu_full = count("gu_full")
        tanh_ready, h_ready, hT_hi, hT_lo = count("tanh_ready"), count("h_ready"), count("hT_hi"), count("hT_lo")
        y_full = count("y_full")
        y_ready, y_stored = count("y_ready"), [count(f"y_stored{u}") for u in range(2)]
        chosen_ready = count("chosen_ready")
        entry_ready, entry_done = count("entry_ready"), [sem(f"entry_done{u}") for u in range(2)]

        xv = d["x"].rearrange("(n t p) c -> n p t c", t=NT, p=P)
        xnv = d["xn_rows"][0:T, :].rearrange("(n t p) c -> n p t c", t=NT, p=P)
        ov = d["out"][0:T, :].rearrange("(n t p) c -> n t p c", t=NT, p=P)
        weights = [(d["sh_gate"].rearrange("(k p) i -> p k i", p=P), sg, I),
                   (d["sh_up"].rearrange("(k p) i -> p k i", p=P), su, I),
                   (d["sh_down"].rearrange("(k p) i -> p k i", p=P), sd, H),
                   (d["wrT2"].rearrange("(k p) i -> p k i", p=P), wr, P)]
        weights += [(d["wT"][j].rearrange("(k p) o -> p k o", p=P), [w[:, j] for w in w_parts], H)
                    for j in range(4)]
        NW = len(weights)
        CONSTS = [(ident, "ident"), (iota_e, "iota_e"), (lower, "lower"), (tok, "tok0"), (spill, "spill0")]

        TP_LOGITS_T, TP_LOGITS, TP_RANK, TP_N = KC, KC + 1, KC + 2, KC + 3

        def tp_use(i, u, k):
            m = TP_N * u + k
            return m % 2, START + 2 * TP_N * i + m + 1

        def tp_released(n, k):
            read, value = [(logits_read, n), (rank_read, n), (xT_lo, KC * n + 1), (xT_lo, KC * n + 2),
                           (xT_lo, KC * n + 3), (xT_lo, KC * n + 4), (lgT_ready, n + 1)][k]
            return read, START + value

        def both(body, eng):
            with eng.Fori(0, B // 2) as i:
                for u in range(2):
                    body(i, u)

        block = ctx.enter_context(nc.Block())

        @block.sync
        def _(sp):
            for s in counts:
                sp.sem_inc(s, START)
            for t, name in CONSTS:
                sp.dma_start(t[:], d[name]).then_inc(const_in, 16)
            sp.dma_start(d["out"][T:T + CAP, :], d["zeros"]).then_inc(init_done, 16)
            for n, (src, parts, width) in enumerate(weights):
                if n:
                    sp.wait_ge(w_hi, n)
                    sp.wait_ge(w_lo, n)
                chunks = src.shape[1]
                sp.dma_start(stage[:, 0:chunks * width].rearrange("p (k n) -> p k n", k=chunks), src)\
                    .then_inc(w_loaded, 16)

            def sequence(i, u):
                n = 2 * i + u
                sp.wait_ge(x_free[u], START + i)
                sp.dma_start(x_in[:, u], xv[bass.ds(n, 1)].rearrange("o p t c -> p (o t) c"))\
                    .then_inc(x_loaded[u], 16)
                sp.wait_ge(xn_ready, START + n + 1)
                sp.dma_start(xnv[bass.ds(n, 1)].rearrange("o p t c -> p (o t) c"), xn[:]).then_inc(xn_stored, 16)
                for t in range(NT):
                    sp.wait_ge(y_ready, START + NT * n + t + 1)
                    sp.dma_start(ov[bass.ds(n, 1), t].rearrange("o p c -> p (o c)"), y_out[:, t % 2])\
                        .then_inc(y_stored[t % 2], 16)

            both(sequence, sp)
            sp.wait_ge(init_done, 16)
            sp.wait_ge(xn_stored, START + 16 * B)
            for u in range(2):
                sp.wait_ge(y_stored[u], START + 16 * B * NT // 2)

        @block.gpsimd
        def _(pool):
            nc.gpsimd.memset(neg_half[:], -0.5).then_inc(pool_const, 1)
            nc.gpsimd.dma_start(d["slots"][0:E * CAP, :], d["slots0"]).then_inc(entry_done[0], FIRST)
            nc.gpsimd.dma_start(d["xn_rows"][T:T + CAP, :], d["zeros"]).then_inc(entry_done[1], FIRST)
            pool.wait_ge(pool_const, 1)
            for u in range(2):
                pool.wait_ge(entry_done[u], FIRST)

            def sequence(i, u):
                n = 2 * i + u
                pool.wait_ge(var_ready, START + n + 1)
                nc.gpsimd.tensor_tensor(rstd[:], veps[:], neg_half[:], ALU.pow).then_inc(rstd_ready, 1)
                pool.wait_ge(entry_ready, START + n + 1)
                nc.gpsimd.tensor_tensor(pool_idle[:], neg_half[:, 0:1], neg_half[:, 1:2], ALU.add)
                for k in range(NT * TOPK):
                    nc.gpsimd.indirect_dma_start(
                        out=d["slots"], out_offset=bass.IndirectOffsetOnAxis(ap=row_u[:, u, k:k + 1], axis=0),
                        in_=entry[:, u, k, :], in_offset=None).then_inc(entry_done[u], 16)

            both(sequence, pool)
            for u in range(2):
                pool.wait_ge(entry_done[u], FIRST + 16 * NT * TOPK * B // 2)

        @block.scalar
        def _(act):
            for n, (src, parts, width) in enumerate(weights):
                split_weights(nc, act, None, stage, [parts[0][:], parts[1][:]], w_loaded, 16 * (n + 1),
                              w_hi, w_lo, n, "act")

            def sequence(i, u):
                n = 2 * i + u
                act.wait_ge(gu_full, START + IC * n)
                for k in range(KC):
                    b, full = tp_use(i, u, k)
                    act.wait_ge(tp_full, full)
                    nc.scalar.activation(xT[0][:, k], tp[b][:], ACT.Copy).then_inc(xT_hi, 1)
                b, full = tp_use(i, u, TP_LOGITS_T)
                act.wait_ge(tp_full, full)
                nc.scalar.activation(lgT[:], tp[b][:], ACT.Copy).then_inc(lgT_ready, 1)

                for c in range(IC):
                    m = IC * u + c
                    act.wait_ge(gu_full, START + 2 * IC * i + m + 1)
                    act.wait_ge(hT_lo, START + 2 * IC * i + max(m - 1, 0))
                    nc.scalar.activation(h[:, m % 2], gt[m % 2][:], ACT.Tanh, scale=0.5).then_inc(tanh_ready, 1)
                    act.wait_ge(h_ready, START + 2 * IC * i + m + 1)
                    if c == 0:
                        act.wait_ge(y_full, START + NT * n)
                    nc.scalar.activation(hT[0][:, c], h[:, m % 2], ACT.Copy).then_inc(hT_hi, 1)
                    if c == 1:
                        act.wait_ge(ex_in, START + n + 1)
                        nc.scalar.activation(ex[:], ex[:], ACT.Exp).then_inc(ex_ready, 1)

            both(sequence, act)

        @block.vector
        def _(dve):
            dve.wait_ge(const_in, 16 * len(CONSTS))
            nc.vector.memset(before[:], 0.0)
            nc.vector.memset(before_b[:], 0.0)
            nc.vector.memset(ones_b[:], 1.0)
            nc.vector.tensor_copy(lower_b[:], lower[:]).then_inc(chosen_ready, 1)
            for n, (src, parts, width) in enumerate(weights):
                split_weights(nc, None, dve, stage, [parts[0][:], parts[1][:]], w_loaded, 16 * (n + 1),
                              w_hi, w_lo, n, "dve")
            CHAIN = 22

            def sequence(i, u):
                n = 2 * i + u
                links = [0]

                def link(ins):
                    links[0] += 1
                    ins.then_inc(dv, 1)
                    dve.wait_ge(dv, START + CHAIN * n + links[0])

                def apart():
                    nc.vector.memset(idle[:], 0.0)

                dve.wait_ge(x_loaded[u], START + 16 * (i + 1))
                for t in range(NT):
                    last = nc.vector.bn_stats(stat[:, t], x_in[:, u, t])
                link(last)
                apart()
                for t in range(NT):
                    last = nc.vector.bn_aggr(mv[:, t], stat[:, t])
                link(last)
                nc.vector.tensor_scalar(veps[:], mv[:, :, 1], EPS, None, ALU.add).then_inc(var_ready, 1)
                dve.wait_ge(rstd_ready, START + n + 1)
                dve.wait_ge(xn_stored, START + 16 * n)
                dve.wait_ge(xT_lo, START + KC * n)
                for t in range(NT):
                    last = nc.vector.tensor_scalar(xn[:, t], x_in[:, u, t], mv[:, t, 0:1], rstd[:, t:t + 1],
                                                   ALU.subtract, ALU.mult)
                last.then_inc(xn_ready, 1)
                for k in range(KC):
                    b, full = tp_use(i, u, k)
                    dve.wait_ge(xT_hi, START + KC * n + k + 1)
                    nc.vector.tensor_tensor(xT[1][:, k], tp[b][:], xT[0][:, k].bitcast(F32), ALU.subtract)\
                        .then_inc(xT_lo, 1)

                def gate(c):
                    m = IC * u + c
                    dve.wait_ge(tanh_ready, START + 2 * IC * i + m + 1)
                    hb = h[:, m % 2]
                    link(nc.vector.scalar_tensor_tensor(out=hb, in0=hb, scalar=1.0, in1=gt[m % 2][:],
                                                        op0=ALU.add, op1=ALU.mult))
                    nc.vector.scalar_tensor_tensor(out=hb, in0=hb, scalar=0.5, in1=up[m % 2][:],
                                                   op0=ALU.mult, op1=ALU.mult)\
                        .then_inc(h_ready, 1)
                    dve.wait_ge(hT_hi, START + 2 * IC * i + m + 1)
                    nc.vector.tensor_tensor(hT[1][:, c], hb, hT[0][:, c].bitcast(F32), ALU.subtract)\
                        .then_inc(hT_lo, 1)

                b, full = tp_use(i, u, TP_LOGITS)
                gate(0)
                dve.wait_ge(tp_full, full)
                link(nc.vector.tensor_copy(lg[:], tp[b][:].rearrange("p (t e) -> p t e", t=NT)[:, :, 0:E]))
                apart()
                for t in range(NT):
                    last = nc.vector.max(top[:, t], lg[:, t])
                link(last)
                apart()
                for t in range(NT):
                    last = nc.vector.max_index(top_i[:, t], top[:, t], lg[:, t])
                last.then_inc(logits_read, 1)
                link(nc.vector.tensor_tensor(ex[:], top[:, :, 0:TOPK], top[:, :, 0:1].to_broadcast([P, NT, TOPK]),
                                             ALU.subtract))
                nc.vector.tensor_copy(idx_f[:].rearrange("p (t j) -> p t j", j=TOPK), top_i[:, :, 0:TOPK])\
                    .then_inc(ex_in, 1)
                dve.wait_ge(ex_in, START + n + 1)
                link(nc.vector.tensor_tensor(onehot[:], iota_e[:].unsqueeze(1).to_broadcast([P, NT * TOPK, E]),
                                             idx_f[:].unsqueeze(2).to_broadcast([P, NT * TOPK, E]), ALU.is_equal))
                oh = onehot[:].rearrange("p (t j) e -> p t j e", j=TOPK)
                pr = prod[:].rearrange("p (t j) e -> p t j e", j=TOPK)
                link(nc.vector.tensor_tensor(pr[:, :, 0:2], oh[:, :, 0:2], oh[:, :, 2:4], ALU.add))
                nc.vector.tensor_tensor(chosen[:], pr[:, :, 0], pr[:, :, 1], ALU.add).then_inc(chosen_ready, 1)
                gate(1)
                dve.wait_ge(ex_ready, START + n + 1)
                link(nc.vector.reduce_sum(esum[:], ex[:], AX_X))
                link(nc.vector.reciprocal(esum[:], esum[:]))
                dve.wait_ge(entry_done[u], FIRST + 16 * NT * TOPK * i)
                nc.vector.tensor_tensor(entry[:, u, :, 1].rearrange("p (t j) -> p t j", j=TOPK), ex[:],
                                        esum[:].unsqueeze(2).to_broadcast([P, NT, TOPK]), ALU.mult)
                link(nc.vector.tensor_copy(entry[:, u, :, 0].rearrange("p (t j) -> p t j", j=TOPK),
                                           tok[:].unsqueeze(2).to_broadcast([P, NT, TOPK])))
                gate(2)
                for t in range(NT):
                    yu = t % 2
                    dve.wait_ge(y_full, START + NT * n + t + 1)
                    dve.wait_ge(y_stored[yu], START + 16 * (2 * n + t // 2))
                    last = nc.vector.tensor_tensor(y_out[:, yu], yb[yu][:], x_in[:, u, t], ALU.add)\
                        .then_inc(y_ready, 1)
                b, full = tp_use(i, u, TP_RANK)
                dve.wait_ge(tp_full, full)
                rank = tp[b][:, 0:NT * E].rearrange("p (t e) -> p t e", e=E)
                nc.vector.tensor_tensor(pr, oh, rank.unsqueeze(2).to_broadcast([P, NT, TOPK, E]), ALU.mult)\
                    .then_inc(rank_read, 1)
                dve.wait_ge(rank_read, START + n + 1)
                link(nc.vector.reduce_sum(place[:], prod[:], AX_X))
                nc.vector.tensor_scalar(fits[:], place[:], float(CAP), None, ALU.is_lt)
                link(nc.vector.scalar_tensor_tensor(out=row[:], in0=idx_f[:], scalar=float(CAP), in1=place[:],
                                                    op0=ALU.mult, op1=ALU.add))
                link(nc.vector.tensor_tensor(row[:], row[:], spill[:], ALU.subtract))
                link(nc.vector.tensor_tensor(row[:], row[:], fits[:], ALU.mult))
                link(nc.vector.tensor_tensor(row[:], row[:], spill[:], ALU.add))
                nc.vector.tensor_copy(row_u[:, u], row[:]).then_inc(entry_ready, 1)
                nc.vector.tensor_scalar(tok[:], tok[:], float(S), None, ALU.add).then_inc(x_free[u], 1)
                nc.vector.tensor_scalar(spill[:], spill[:], float(S * TOPK), None, ALU.add)
                link(nc.vector.tensor_tensor(pr[:, 0:2, 0], chosen[:, 0:2], chosen[:, 2:4], ALU.add))
                link(nc.vector.tensor_tensor(chosen_sum[:], pr[:, 0, 0], pr[:, 1, 0], ALU.add))
                link(nc.vector.tensor_tensor(before[:], before[:], chosen_sum[:], ALU.add))
                link(nc.vector.tensor_copy(before_b[:], before[:]))
                assert links[0] == CHAIN, links[0]

            both(sequence, dve)

        @block.tensor
        def _(pe):
            pe.wait_ge(const_in, 16 * len(CONSTS))
            pe.wait_ge(w_lo, NW)
            pe.wait_ge(chosen_ready, START + 1)

            def sequence(i, u):
                n = 2 * i + u
                pe.wait_ge(xn_ready, START + n + 1)
                for k in range(KC):
                    b, _ = tp_use(i, u, k)
                    pe.wait_ge(*tp_released(n, k))
                    for t in range(NT):
                        last = nc.tensor.transpose(tp[b][:, t * P:(t + 1) * P], xn[:, t, k * P:(k + 1) * P], ident[:])
                    last.then_inc(tp_full, 1)
                pe.wait_ge(xT_lo, START + KC * (n + 1))
                b, _ = tp_use(i, u, TP_LOGITS_T)
                pe.wait_ge(*tp_released(n, TP_LOGITS_T))
                three_products(nc, tp[b][:], lambda a, k: wr[a][:, k], lambda a, k: xT[a][:, k], range(KC))\
                    .then_inc(tp_full, 1)
                for c in range(IC):
                    m = IC * u + c
                    pe.wait_ge(h_ready, START + 2 * IC * i + max(m - 1, 0))
                    for w, bank in ((sg, gt), (su, up)):
                        last = three_products(nc, bank[m % 2][:], lambda a, k: w[a][:, k, c * P:(c + 1) * P],
                                              lambda a, k: xT[a][:, k], range(KC))
                    last.then_inc(gu_full, 1)
                    if c == 0:
                        b, _ = tp_use(i, u, TP_LOGITS)
                        pe.wait_ge(lgT_ready, START + n + 1)
                        pe.wait_ge(*tp_released(n, TP_LOGITS))
                        for t in range(NT):
                            last = nc.tensor.transpose(tp[b][:, t * P:(t + 1) * P], lgT[:, t * P:(t + 1) * P], ident[:])
                        last.then_inc(tp_full, 1)
                last = None
                b, _ = tp_use(i, u, TP_RANK)
                pe.wait_ge(*tp_released(n, TP_RANK))
                pe.wait_ge(chosen_ready, START + n + 2)
                pe.wait_ge(gu_full, START + 2 * IC * i + IC * (u + 1))
                rank = tp[b][:, 0:NT * E]
                nc.tensor.matmul(rank, lower_b[:], chosen[:].rearrange("p t e -> p (t e)"), start=True, stop=False)
                for t in range(NT - 1):
                    later = NT - 1 - t
                    nc.tensor.matmul(tp[b][:, (t + 1) * E:NT * E], ones_b[:],
                                     chosen[:, t:t + 1].to_broadcast([P, later, E]), start=False, stop=False)
                nc.tensor.matmul(rank, ones_b[:], before_b[:].unsqueeze(1).to_broadcast([P, NT, E]),
                                 start=False, stop=True).then_inc(tp_full, 1)
                for t in range(NT):
                    yu = t % 2
                    if t == 0:
                        pe.wait_ge(hT_lo, START + IC * (n + 1))
                    pe.wait_ge(y_ready, START + NT * n + max(t - 1, 0))
                    last = three_products(nc, yb[yu][:], lambda a, c: hT[a][:, c, t * P:(t + 1) * P],
                                          lambda a, c: sd[a][:, c], range(IC))
                    last.then_inc(y_full, 1)

            both(sequence, pe)


def stage_two(nc, d, ident, w_parts):
    with ExitStack() as ctx:
        def sb(name, shape, dt=F32):
            return ctx.enter_context(nc.sbuf_tensor(name, shape, dt))

        def sem(name):
            return ctx.enter_context(nc.semaphore(name))

        counts = []

        def count(name):
            counts.append(sem(name))
            return counts[-1]

        def bank(name):
            return ctx.enter_context(nc.psum_tensor(name, [P, 512], F32))

        ring = [bank(f"ring{j}") for j in range(4)]
        o_bank, sum_bank = bank("o_bank"), bank("sum_bank")
        ea, eb = bank("ea"), bank("eb")

        xt = [sb(f"xt{j}", [P, H]) for j in range(2)]
        xo = [sb(f"xo_{a}", [P, KC, S], F32R) for a in "hl"]
        qk = sb("qk", [P, 2, NT, H])
        v = sb("v", [P, NT, H])
        t1 = sb("t1", [P, H])
        t2 = sb("t2", [P, H])
        parts = sb("parts", [P, 2, NT, GH, SPLIT], F32R)
        stacks = [sb(f"stack_{a}", [P, GH, S], F32R) for a in "qk"]
        prob = sb("prob", [P, GH, PW])
        wo_out = [sb(f"wo_out{j}", [P, H]) for j in range(2)]
        wgu = sb("wgu", [P, 2, 2, KC, I])
        wdn = sb("wdn", [P, 2, IC, H])
        xe = sb("xe", [P, H])
        xeT = sb("xeT", [P, KC, P])
        he = sb("he", [P, I])
        heT = sb("heT", [P, IC, P])
        ye = sb("ye", [P, H])
        cos, sin = sb("cos", [P, NT, HD]), sb("sin", [P, NT, HD])
        mask = sb("mask", [P, S], BF16)
        ones = sb("ones", [P, HD])
        peak = sb("peak", [P, NT, GH])
        shift = sb("shift", [P, NT, GH, HD], F32R)
        table = sb("table", [P, E // 2, 2])
        table_s = sb("table_s", [CAP, E, 2])
        row_g = sb("row_g", [P, E // 2], U32)
        row_s = sb("row_s", [CAP, E], U32)
        now_g = sb("now_g", [P, 1], U32)
        now_s = sb("now_s", [CAP, 2], U32)
        pool_zero = sb("pool_zero", [P, 2])
        pool_idle = sb("pool_idle2", [P, 48])
        idle = sb("idle2", [P, 10 * NG])

        const_in, const_set, pool_const = sem("const_in2"), sem("const_set"), sem("pool_const2")
        table_in, table_ready = sem("table_in"), sem("table_ready")
        xt_in, xt_used = [count(f"xt_in{j}") for j in range(2)], count("xt_used")
        ring_full = count("ring_full")
        xo_hi, xo_lo = count("xo_hi"), count("xo_lo")
        rope_1, rope_2, rope_read, qk_ready, v_ready = (count(s) for s in ("rope_1", "rope_2", "rope_read", "qk_ready", "v_ready"))
        part_hi, part_dup, part_lo = count("part_hi"), count("part_dup"), count("part_lo")
        q_ready, k_ready = count("q_ready"), count("k_ready")
        s_read, shift_hi, shift_lo, shift_in = count("s_read"), count("shift_hi"), count("shift_lo"), count("shift_in")
        exp_done, masked, pv_done = count("exp_done"), count("masked"), count("pv_done")
        o_inv, o_ready, o_hi, o_lo = count("o_inv"), count("o_ready"), count("o_hi"), count("o_lo")
        wo_ready = count("wo_ready")
        gu_in, dn_in = count("gu_in"), count("dn_in")
        xe_in, xeT_full, xeT_ready = sem("xe_in"), count("xeT_full"), count("xeT_ready")
        gu_full, tanh_ready, gated, he_ready = count("gu_full2"), count("tanh_ready2"), count("gated"), count("he_ready")
        heT_full, heT_ready, ye_full, ye_ready = count("heT_full"), count("heT_ready"), count("ye_full"), count("ye_ready")
        now_set, added = count("now_set"), sem("added")

        def s_pieces(width):
            full, three, two, one = (sorted(range(NT), key=lambda t: -width[t]))
            out = []
            for hh in range(2):
                out.append([(hh, full, 0, width[full])])
                out.append([(hh, three, 0, width[three]), (hh, one, width[three], width[one])])
            out.append([(hh, two, hh * width[two], width[two]) for hh in range(2)])
            return out

        S_PIECES = s_pieces([P * (t + 1) for t in range(NT)])
        T_PIECES = s_pieces([P * (NT - t) for t in range(NT)])
        EXPS = sum(len(x) for x in T_PIECES)

        uses = [(("x", k), xo_lo, k + 1) for k in range(KC)]
        uses += [(("qk", t, j), rope_read, 2 * t + j + 1) for t in range(NT) for j in range(2)]
        uses += [(("v", t), v_ready, t + 1) for t in range(NT)]

        def stack_uses(g):
            return [(("stack", g, h, j), (q_ready, k_ready)[j], GH * g + h + 1) for h in range(GH) for j in range(2)]

        uses += stack_uses(0)
        for g in range(NG):
            for pair in range(2):
                uses += [(("s", g, pair, m), s_read, 10 * g + 5 * pair + m + 1) for m in range(5)]
            uses += [(("shift", g), shift_in, GH * (g + 1))]
            for pair in range(2):
                done = EXPS * (2 * g + pair)
                for m in range(5):
                    done += len(T_PIECES[m])
                    uses += [(("t", g, pair, m), exp_done, done)]
            if g < NG - 1:
                uses += stack_uses(g + 1)
        uses += [(("wo", t), wo_ready, t + 1) for t in range(NT)]
        RING_N = len(uses)
        number = {name: m for m, (name, _, _) in enumerate(uses)}
        assert RING_N % 4 == 0
        each = {xo_lo: KC, rope_read: 2 * NT, v_ready: NT, q_ready: NH, k_ready: NH, s_read: 10 * NG,
                shift_in: GH * NG, exp_done: EXPS * 2 * NG, wo_ready: NT}

        def bank_of(*name):
            return ring[number[name] % 4]

        def full(i, *name):
            return ring_full, START + RING_N * i + number[name] + 1

        def released(i, *name):
            m = number[name]
            if m < 4:
                return wo_ready, START + NT * i
            _, s, value = uses[m - 4]
            return s, START + each[s] * i + value

        xnv = d["xn_rows"][0:T, :].rearrange("(n t p) c -> n t p c", t=NT, p=P)
        ov = d["out"][0:T, :].rearrange("(n t p) c -> n t p c", t=NT, p=P)
        gv = [d[n].rearrange("e (k p) i -> e p k i", p=P) for n in ("w_gate", "w_up")]
        dv_ = d["w_down"].rearrange("e (k p) i -> e p k i", p=P)

        block = ctx.enter_context(nc.Block())

        @block.sync
        def _(sp):
            for s in counts:
                sp.sem_inc(s, START)
            sp.dma_start(cos[:], d["cos"]).then_inc(const_in, 16)
            sp.dma_start(sin[:], d["sin"]).then_inc(const_in, 16)
            lists = d["slots"][0:E * CAP, :]
            sp.dma_start(table[:], lists.rearrange("(q p) c -> p q c", p=P)).then_inc(table_in, 16)
            sp.dma_start(table_s[:], lists.rearrange("(e p) c -> p e c", p=CAP)).then_inc(table_in, 16)

            with sp.Fori(0, B) as i:
                def rows(t):
                    if t < 2:
                        sp.wait_ge(ring_full, START + RING_N * i)
                    else:
                        sp.wait_ge(xt_used, START + 3 * i + t - 1)
                    sp.dma_start(xt[t % 2][:], xnv[bass.ds(i, 1), t].rearrange("o p c -> p (o c)"))\
                        .then_inc(xt_in[t % 2], 16)

                def gate_up(g):
                    sp.wait_ge(gu_full, START + PAIRS * i + g)
                    for ab in range(2):
                        for w in range(2):
                            sp.dma_start(wgu[:, w, ab], gv[w][bass.ds(i * 2 * PAIRS + (2 * g + ab), 1)]
                                         .rearrange("e p k i -> p (e k) i")).then_inc(gu_in, 16)

                def down(g):
                    sp.wait_ge(ye_full, START + PAIRS * i + g)
                    for ab in range(2):
                        sp.dma_start(wdn[:, ab], dv_[bass.ds(i * 2 * PAIRS + (2 * g + ab), 1)]
                                     .rearrange("e p k i -> p (e k) i")).then_inc(dn_in, 16)

                rows(0)
                rows(1)
                rows(2)
                rows(3)
                for g in range(NG):
                    gate_up(g)
                    down(g)

        @block.gpsimd
        def _(pool):
            nc.gpsimd.memset(pool_zero[:], 0.0).then_inc(pool_const, 1)
            pool.wait_ge(pool_const, 1)
            nc.gpsimd.dma_start(t1[:], d["mask"]).then_inc(added, FIRST)
            pool.wait_ge(table_ready, 1)

            def take_wait():
                n = next(pool_cells)
                nc.gpsimd.tensor_tensor(pool_idle[:, n:n + 1], pool_zero[:, 0:1], pool_zero[:, 1:2], ALU.add)

            pool_cells = iter(range(pool_idle.shape[1]))

            with pool.Fori(0, B) as i:
                NOW = 2 * PAIRS
                now_count = iter(range(1, NOW + 1))

                def gather(g):
                    pool.wait_ge(xeT_full, START + PAIRS * i + g)
                    take_wait()
                    nc.gpsimd.tensor_copy(now_g[:], row_g[:, bass.ds(i * PAIRS + g, 1)]).then_inc(now_set, 1)
                    pool.wait_ge(now_set, START + NOW * i + next(now_count))
                    take_wait()
                    nc.gpsimd.indirect_dma_start(
                        out=xe[:], out_offset=None, in_=d["xn_rows"],
                        in_offset=bass.IndirectOffsetOnAxis(ap=now_g[:], axis=0)).then_inc(xe_in, 16)

                def scatter(g):
                    pool.wait_ge(ye_ready, START + PAIRS * i + g + 1)
                    pool.wait_ge(added, FIRST + 16 * (12 * i + 2 * g))
                    take_wait()
                    nc.gpsimd.tensor_copy(now_s[:], row_s[:, bass.ds((i * PAIRS + g) * 2, 2)]).then_inc(now_set, 1)
                    pool.wait_ge(now_set, START + NOW * i + next(now_count))
                    take_wait()
                    for ab in range(2):
                        if ab:
                            pool.wait_ge(added, FIRST + 16 * (12 * i + 2 * g + 1))
                            take_wait()
                        nc.gpsimd.indirect_dma_start(
                            out=d["out"], out_offset=bass.IndirectOffsetOnAxis(ap=now_s[:, ab:ab + 1], axis=0),
                            in_=ye[ab * CAP:(ab + 1) * CAP, :], in_offset=None,
                            compute_op=ALU.add).then_inc(added, 16)

                def duplicate(g):
                    for j in range(2):
                        pool.wait_ge(part_hi, START + 2 * NG * i + 2 * g + j + 1)
                        take_wait()
                        to = parts[:, j, :, :, HD * (1 + j):HD * (2 + j)]
                        nc.gpsimd.tensor_copy(to, parts[:, j, :, :, 0:HD].bitcast(F32)).then_inc(part_dup, 1)

                def causal(g, pair):
                    pool.wait_ge(exp_done, START + EXPS * (2 * NG * i + 2 * g + pair + 1))
                    take_wait()
                    for h in (2 * pair, 2 * pair + 1):
                        for view in (prob[:, h, 0:1024].rearrange("p (a b) -> p a b", a=2)[:, :, 0:P],
                                     prob[:, h, 896:1152].rearrange("p (a b) -> p a b", a=2)):
                            nc.gpsimd.affine_select(out=view, in_=view, compare_op=ALU.is_ge, fill=0.0, base=0,
                                                    pattern=[[0, 2], [1, P]], channel_multiplier=-1)\
                                .then_inc(masked, 1)

                gather(0)
                duplicate(0)
                for g in range(NG):
                    if g < NG - 1:
                        gather(g + 1)
                    if g:
                        scatter(g - 1)
                    causal(g, 0)
                    if g < NG - 1:
                        duplicate(g + 1)
                    causal(g, 1)
                scatter(NG - 1)
                for t in range(NT):
                    pool.wait_ge(wo_ready, START + NT * i + t + 1)
                    pool.wait_ge(added, FIRST + 16 * (12 * i + 8 + t))
                    take_wait()
                    nc.gpsimd.dma_start(ov[bass.ds(i, 1), t].rearrange("o p c -> p (o c)"), wo_out[t % 2][:],
                                        accum_op=ALU.add).then_inc(added, 16)
            pool.wait_ge(added, FIRST + 16 * 12 * B)

        @block.scalar
        def _(act):
            with act.Fori(0, B) as i:
                def split(g):
                    for j in range(2):
                        act.wait_ge(qk_ready, START + 2 * NT * (i + 1))
                        if g:
                            act.wait_ge(*full(i, "stack", g - 1, GH - 1, j))
                        else:
                            act.wait_ge(*full(i, "x", KC - 1))
                        nc.scalar.activation(parts[:, j, :, :, 0:HD],
                                             qk[:, j, :, g * P:(g + 1) * P].rearrange("p t (h e) -> p t h e", e=HD),
                                             ACT.Copy).then_inc(part_hi, 1)

                def stack(g):
                    for h in range(GH):
                        act.wait_ge(*full(i, "stack", g, h, 0))
                        nc.scalar.activation(stacks[0][0:SPLIT, h], bank_of("stack", g, h, 0)[0:SPLIT, :],
                                             ACT.Copy).then_inc(q_ready, 1)

                def exps(g, pair):
                    if pair == 0:
                        act.wait_ge(pv_done, START + NG * i + g)
                    for m, piece in enumerate(T_PIECES):
                        act.wait_ge(*full(i, "t", g, pair, m))
                        for hh, t, col, width in piece:
                            nc.scalar.activation(prob[:, 2 * pair + hh, KOFF[t]:KOFF[t] + width],
                                                 bank_of("t", g, pair, m)[:, col:col + width], ACT.Exp,
                                                 scale=SCALE).then_inc(exp_done, 1)

                def heads_out(g):
                    act.wait_ge(o_ready, START + NG * i + g + 1)
                    nc.scalar.activation(xo[0][:, g], t2[:], ACT.Copy).then_inc(o_hi, 1)

                for k in range(KC):
                    act.wait_ge(*full(i, "x", KC - 1))
                    nc.scalar.activation(xo[0][:, k], bank_of("x", k)[:], ACT.Copy).then_inc(xo_hi, 1)
                for t in range(NT):
                    act.wait_ge(*full(i, "v", t))
                    if t == 0:
                        act.wait_ge(pv_done, START + NG * i)
                    nc.scalar.activation(v[:, t], bank_of("v", t)[:], ACT.Copy).then_inc(v_ready, 1)
                    if t == 0:
                        split(0)
                stack(0)
                for g in range(NG):
                    act.wait_ge(xeT_full, START + PAIRS * i + g + 1)
                    nc.scalar.activation(xeT[:].rearrange("p k n -> p (k n)"), ea[:], ACT.Copy).then_inc(xeT_ready, 1)
                    if g:
                        heads_out(g - 1)
                    act.wait_ge(*full(i, "shift", g))
                    for h in range(GH):
                        nc.scalar.activation(stacks[0][SPLIT:SHIFT, h], bank_of("shift", g)[HD * h:HD * h + 2, :],
                                             ACT.Copy).then_inc(shift_in, 1)
                    exps(g, 0)
                    if g < NG - 1:
                        split(g + 1)
                    act.wait_ge(gu_full, START + PAIRS * i + g + 1)
                    act.wait_ge(heT_full, START + PAIRS * i + g)
                    nc.scalar.activation(he[:], ea[:, 0:I], ACT.Tanh, scale=0.5).then_inc(tanh_ready, 1)
                    exps(g, 1)
                    if g < NG - 1:
                        stack(g + 1)
                    act.wait_ge(heT_full, START + PAIRS * i + g + 1)
                    nc.scalar.activation(heT[:].rearrange("p k n -> p (k n)"), ea[:, 0:I], ACT.Copy)\
                        .then_inc(heT_ready, 1)
                heads_out(NG - 1)
                for t in range(NT):
                    act.wait_ge(*full(i, "wo", t))
                    act.wait_ge(added, FIRST + 16 * (12 * i + (0 if t < 2 else 8 + t - 1)))
                    nc.scalar.activation(wo_out[t % 2][:], bank_of("wo", t)[:], ACT.Copy).then_inc(wo_ready, 1)

        @block.vector
        def _(dve):
            dve.wait_ge(table_in, 32)
            nc.vector.tensor_copy(row_g[:], table[:, :, 0])
            nc.vector.tensor_copy(row_s[:], table_s[:, :, 0]).then_inc(table_ready, 1)
            dve.wait_ge(const_in, 2 * 16)
            dve.wait_ge(added, FIRST)
            nc.vector.tensor_copy(mask[:], t1[:])
            nc.vector.memset(ones[:], 1.0)
            nc.vector.memset(shift[:].bitcast(F32), 0.0)
            nc.vector.memset(stacks[1][SPLIT:SHIFT].bitcast(F32), 1.0).then_inc(const_set, 1)
            dve.wait_ge(const_set, 1)

            with dve.Fori(0, B) as i:
                def split(g):
                    for j in range(2):
                        dve.wait_ge(part_hi, START + 2 * NG * i + 2 * g + j + 1)
                        nc.vector.tensor_tensor(parts[:, j, :, :, HD * (2 - j):HD * (3 - j)],
                                                qk[:, j, :, g * P:(g + 1) * P].rearrange("p t (h e) -> p t h e", e=HD),
                                                parts[:, j, :, :, 0:HD].bitcast(F32), ALU.subtract)\
                            .then_inc(part_lo, 1)

                def stack(g):
                    for h in range(GH):
                        dve.wait_ge(*full(i, "stack", g, h, 1))
                        nc.vector.tensor_copy(stacks[1][0:SPLIT, h], bank_of("stack", g, h, 1)[0:SPLIT, :])\
                            .then_inc(k_ready, 1)

                def peaks(g, pair):
                    for m, piece in enumerate(S_PIECES):
                        dve.wait_ge(*full(i, "s", g, pair, m))
                        nc.vector.memset(idle[:, 10 * g + 5 * pair + m:10 * g + 5 * pair + m + 1], 0.0)
                        for hh, t, col, width in piece:
                            part = bank_of("s", g, pair, m)[:, col:col + width]
                            last = nc.vector.tensor_tensor_reduce(
                                out=part, in0=part, in1=mask[:, S - width:S], scale=1.0, scalar=-3e38,
                                op0=ALU.add, op1=ALU.max, accum_out=peak[:, t, 2 * pair + hh:2 * pair + hh + 1])
                        last.then_inc(s_read, 1)

                def heads_out(g):
                    dve.wait_ge(pv_done, START + NG * i + g + 1)
                    nc.vector.reciprocal(t1[:], sum_bank[:]).then_inc(o_inv, 1)
                    dve.wait_ge(o_inv, START + NG * i + g + 1)
                    nc.vector.tensor_tensor(t2[:], o_bank[:], t1[:], ALU.mult).then_inc(o_ready, 1)
                    dve.wait_ge(o_hi, START + NG * i + g + 1)
                    nc.vector.tensor_tensor(xo[1][:, g], t2[:], xo[0][:, g].bitcast(F32), ALU.subtract)\
                        .then_inc(o_lo, 1)

                def expert_out(g):
                    dve.wait_ge(ye_full, START + PAIRS * i + g + 1)
                    dve.wait_ge(added, FIRST + 16 * (12 * i + 2 * g))
                    nc.vector.tensor_scalar(ye[:], eb[:], table[:, bass.ds(i * PAIRS + g, 1), 1], None, ALU.mult)\
                        .then_inc(ye_ready, 1)

                for k in range(KC):
                    dve.wait_ge(xo_hi, START + KC * i + k + 1)
                    nc.vector.tensor_tensor(xo[1][:, k], bank_of("x", k)[:], xo[0][:, k].bitcast(F32), ALU.subtract)\
                        .then_inc(xo_lo, 1)
                for t in range(NT):
                    for j in range(2):
                        n = 2 * NT * i + 2 * t + j + 1
                        dve.wait_ge(*full(i, "qk", t, j))
                        dve.wait_ge(qk_ready, START + n - 1)
                        b = bank_of("qk", t, j)[:].rearrange("p (h e) -> p h e", e=HD)
                        a1, a2 = (x[:].rearrange("p (h e) -> p h e", e=HD) for x in (t1, t2))
                        nc.vector.tensor_tensor(a1, b, cos[:, t:t + 1, :].to_broadcast([P, NH, HD]), ALU.mult)
                        nc.vector.tensor_tensor(a2[:, :, 0:HD // 2], b[:, :, HD // 2:HD],
                                                sin[:, t:t + 1, 0:HD // 2].to_broadcast([P, NH, HD // 2]), ALU.mult)
                        nc.vector.tensor_tensor(a2[:, :, HD // 2:HD], b[:, :, 0:HD // 2],
                                                sin[:, t:t + 1, HD // 2:HD].to_broadcast([P, NH, HD // 2]), ALU.mult)\
                            .then_inc(rope_read, 1)
                        dve.wait_ge(rope_read, START + n)
                        nc.vector.tensor_tensor(qk[:, j, t], t1[:], t2[:], ALU.add).then_inc(qk_ready, 1)
                split(0)
                stack(0)
                for g in range(NG):
                    peaks(g, 0)
                    peaks(g, 1)
                    n = NG * i + g + 1
                    dve.wait_ge(s_read, START + 10 * n)
                    dve.wait_ge(*full(i, "stack", g, GH - 1, 1))
                    nc.vector.tensor_scalar(shift[:, :, :, 0], peak[:], -1.0, None, ALU.mult).then_inc(shift_hi, 1)
                    dve.wait_ge(shift_hi, START + n)
                    nc.vector.scalar_tensor_tensor(out=shift[:, :, :, 1], in0=peak[:], scalar=-1.0,
                                                   in1=shift[:, :, :, 0].bitcast(F32), op0=ALU.mult,
                                                   op1=ALU.subtract).then_inc(shift_lo, 1)
                    if g:
                        heads_out(g - 1)
                        expert_out(g - 1)
                    if g < NG - 1:
                        split(g + 1)
                    dve.wait_ge(tanh_ready, START + n)
                    nc.vector.scalar_tensor_tensor(out=he[:], in0=he[:], scalar=1.0, in1=ea[:, 0:I],
                                                   op0=ALU.add, op1=ALU.mult).then_inc(gated, 1)
                    dve.wait_ge(gated, START + n)
                    nc.vector.scalar_tensor_tensor(out=he[:], in0=he[:], scalar=0.5, in1=eb[:, 0:I],
                                                   op0=ALU.mult, op1=ALU.mult).then_inc(he_ready, 1)
                    if g < NG - 1:
                        stack(g + 1)
                heads_out(NG - 1)
                expert_out(NG - 1)

        @block.tensor
        def _(pe):
            pe.wait_ge(const_set, 1)

            with pe.Fori(0, B) as i:
                def acquire(*name):
                    pe.wait_ge(*released(i, *name))
                    return bank_of(*name)

                def stack(g):
                    for h in range(GH):
                        for j in range(2):
                            pe.wait_ge(part_dup, START + 2 * NG * i + 2 * g + j + 1)
                            pe.wait_ge(part_lo, START + 2 * NG * i + 2 * g + j + 1)
                            b = acquire("stack", g, h, j)
                            for t in range(NT):
                                last = nc.tensor.transpose(b[0:SPLIT, t * P:(t + 1) * P],
                                                           parts[:, j, t, h].bitcast(F32), ident[:])
                            last.then_inc(ring_full, 1)

                def scores(g, pair):
                    if pair == 0:
                        pe.wait_ge(q_ready, START + GH * (NG * i + g + 1))
                        pe.wait_ge(k_ready, START + GH * (NG * i + g + 1))
                    for m, piece in enumerate(S_PIECES):
                        b = acquire("s", g, pair, m)
                        for hh, t, col, width in piece:
                            h = 2 * pair + hh
                            last = nc.tensor.matmul(b[:, col:col + width], stacks[0][0:SPLIT, h, t * P:(t + 1) * P],
                                                    stacks[1][0:SPLIT, h, 0:width], start=True, stop=True)
                        last.then_inc(ring_full, 1)

                def scores_t(g, pair):
                    for m, piece in enumerate(T_PIECES):
                        b = acquire("t", g, pair, m)
                        if pair == 0 and m == 0:
                            pe.wait_ge(shift_in, START + GH * (NG * i + g + 1))
                        for hh, t, col, width in piece:
                            h = 2 * pair + hh
                            last = nc.tensor.matmul(b[:, col:col + width], stacks[1][0:SHIFT, h, t * P:(t + 1) * P],
                                                    stacks[0][0:SHIFT, h, S - width:S], start=True, stop=True)
                        last.then_inc(ring_full, 1)

                def shifts(g):
                    pe.wait_ge(shift_lo, START + NG * i + g + 1)
                    b = acquire("shift", g)
                    for t in range(NT):
                        last = nc.tensor.transpose(b[:, t * P:(t + 1) * P],
                                                   shift[:, t].rearrange("p h e -> p (h e)").bitcast(F32), ident[:])
                    last.then_inc(ring_full, 1)

                def values(g):
                    pe.wait_ge(masked, START + 2 * GH * (NG * i + g + 1))
                    pe.wait_ge(o_ready, START + NG * i + g)
                    for out, left in ((o_bank, None), (sum_bank, ones)):
                        for t in range(NT):
                            for h in range(GH):
                                w = v[:, t, (GH * g + h) * HD:(GH * g + h + 1) * HD] if left is None else left[:]
                                last = nc.tensor.matmul(out[h * HD:(h + 1) * HD, t * P:S], w,
                                                        prob[:, h, KOFF[t]:KOFF[t] + S - t * P],
                                                        start=(t == 0), stop=(t == NT - 1),
                                                        skip_group_check=True)
                    last.then_inc(pv_done, 1)

                def expert_rows(g):
                    pe.wait_ge(xe_in, 16 * (PAIRS * i + g + 1))
                    pe.wait_ge(heT_ready, START + PAIRS * i + g)
                    for k in range(KC):
                        last = nc.tensor.transpose(ea[:, k * P:(k + 1) * P], xe[:, k * P:(k + 1) * P], ident[:])
                    last.then_inc(xeT_full, 1)

                def expert_gate_up(g):
                    pe.wait_ge(xeT_ready, START + PAIRS * i + g + 1)
                    pe.wait_ge(ye_ready, START + PAIRS * i + g)
                    pe.wait_ge(gu_in, START + 64 * (PAIRS * i + g + 1))
                    for k in range(KC):
                        for w, b in ((0, ea), (1, eb)):
                            for ab in range(2):
                                last = nc.tensor.matmul(b[ab * CAP:(ab + 1) * CAP, 0:I],
                                                        xeT[:, k, ab * CAP:(ab + 1) * CAP], wgu[:, w, ab, k],
                                                        start=(k == 0), stop=(k == KC - 1), skip_group_check=True)
                    last.then_inc(gu_full, 1)

                def expert_turn(g):
                    pe.wait_ge(he_ready, START + PAIRS * i + g + 1)
                    for c in range(IC):
                        last = nc.tensor.transpose(ea[:, c * P:(c + 1) * P], he[:, c * P:(c + 1) * P], ident[:])
                    last.then_inc(heT_full, 1)

                def expert_down(g):
                    pe.wait_ge(heT_ready, START + PAIRS * i + g + 1)
                    pe.wait_ge(dn_in, START + 32 * (PAIRS * i + g + 1))
                    for c in range(IC):
                        for ab in range(2):
                            last = nc.tensor.matmul(eb[ab * CAP:(ab + 1) * CAP, :], heT[:, c, ab * CAP:(ab + 1) * CAP],
                                                    wdn[:, ab, c], start=(c == 0), stop=(c == IC - 1),
                                                    skip_group_check=True)
                    last.then_inc(ye_full, 1)

                for k in range(KC):
                    acquire("x", k)
                for t in range(NT):
                    pe.wait_ge(xt_in[t % 2], START + 16 * (2 * i + t // 2 + 1))
                    for k in range(KC):
                        last = nc.tensor.transpose(bank_of("x", k)[:, t * P:(t + 1) * P],
                                                   xt[t % 2][:, k * P:(k + 1) * P], ident[:])
                        if t == NT - 1:
                            last.then_inc(ring_full, 1)
                    if t < NT - 1:
                        last.then_inc(xt_used, 1)
                pe.wait_ge(xo_lo, START + KC * (i + 1))
                for t, j in [(t, j) for t in range(NT) for j in range(2)] + [(t, 2) for t in range(NT)]:
                    b = acquire("qk", t, j) if j < 2 else acquire("v", t)
                    three_products(nc, b[:], lambda a, k: xo[a][:, k, t * P:(t + 1) * P],
                                   lambda a, k: w_parts[a][:, j, k], range(KC)).then_inc(ring_full, 1)
                stack(0)
                for g in range(NG):
                    scores(g, 0)
                    expert_rows(g)
                    scores(g, 1)
                    if g:
                        values(g - 1)
                        expert_down(g - 1)
                    shifts(g)
                    scores_t(g, 0)
                    expert_gate_up(g)
                    scores_t(g, 1)
                    if g < NG - 1:
                        stack(g + 1)
                    expert_turn(g)
                values(NG - 1)
                expert_down(NG - 1)
                pe.wait_ge(o_lo, START + NG * (i + 1))
                for t in range(NT):
                    b = acquire("wo", t)
                    three_products(nc, b[:], lambda a, g: xo[a][:, g, t * P:(t + 1) * P],
                                   lambda a, g: w_parts[a][:, 3, g], range(NG)).then_inc(ring_full, 1)


_OUT_ROWS = T + CAP


def _constants():
    p = np.arange(P, dtype=np.float32)
    c = {}
    c["ident"] = np.eye(P, dtype=np.float32)
    c["iota_e"] = np.tile(np.arange(E, dtype=np.float32), (P, 1))
    c["lower"] = (p[:, None] < p[None, :]).astype(np.float32)
    c["tok0"] = p[:, None] + P * np.arange(NT, dtype=np.float32)[None, :]
    c["spill0"] = np.float32(E * CAP) + p[:, None] * (NT * TOPK) + np.arange(NT * TOPK, dtype=np.float32)[None, :]
    slots = np.zeros((E, CAP, 2), np.float32)
    slots[:, :, 0] = T + np.arange(CAP)
    c["slots0"] = slots.reshape(E * CAP, 2)
    c["zeros"] = np.zeros((CAP, H), np.float32)
    inv_freq = 1.0 / 10000.0 ** (np.arange(0, HD, 2, dtype=np.float32) / HD)
    freqs = np.einsum("i,j->ij", np.arange(S, dtype=np.float32), inv_freq)
    emb = np.concatenate((freqs, freqs), axis=-1)
    sign = np.where(np.arange(HD) < HD // 2, np.float32(-1), np.float32(1))
    c["cos"] = np.ascontiguousarray(np.cos(emb).astype(np.float32).reshape(NT, P, HD).transpose(1, 0, 2))
    c["sin"] = np.ascontiguousarray((np.sin(emb).astype(np.float32) * sign).reshape(NT, P, HD).transpose(1, 0, 2))
    mask = np.zeros((P, S), np.float32)
    mask[:, S - P:] = np.where(p[None, :] <= p[:, None], 0.0, -1e30)
    c["mask"] = mask
    return c


def kernel(**inputs):
    import concourse.bacc as _bacc
    from concourse.bass_utils import run_bass_kernel_spmd as _run

    g = {k: np.asarray(v) for k, v in inputs.items()}
    arrays = {
        "x": g["L0_attn_hidden_states"].reshape(T, H),
        "wT": np.stack([g[f"L0_attn_W{n}"].T for n in "qkvo"]),
        "wrT2": np.concatenate([g["L0_ffn_w_router"].T] * 2, axis=1),
        "sh_gate": g["L0_ffn_w_sh_gate"], "sh_up": g["L0_ffn_w_sh_up"], "sh_down": g["L0_ffn_w_sh_down"],
        "w_gate": g["L0_ffn_w_gate"], "w_up": g["L0_ffn_w_up"], "w_down": g["L0_ffn_w_down"],
    }
    arrays.update(_constants())
    arrays = {k: np.ascontiguousarray(v) for k, v in arrays.items()}
    nc = _bacc.Bacc("TRN2", target_bir_lowering=False, num_devices=1,
                    dynamic_dma_scratch_size=8192)
    d = {k: nc.dram_tensor(f"in_{k}", v.shape, mybir.dt.from_np(v.dtype), kind="ExternalInput").ap()
         for k, v in arrays.items()}
    d["out"] = nc.dram_tensor("out_rows", [_OUT_ROWS, H], F32, kind="ExternalOutput").ap()
    d["xn_rows"] = nc.dram_tensor("xn_rows", [T + CAP, H], F32).ap()
    d["slots"] = nc.dram_tensor("slots", [E * CAP + T * TOPK, 2], F32).ap()
    build(nc, d)
    r = _run(nc, [{f"in_{k}": v for k, v in arrays.items()}], core_ids=[0])
    return r.results[0]["out_rows"][0:T].reshape(B, S, H)
```

```python
from contextlib import ExitStack

import numpy as np

import concourse.bass as bass
from concourse import mybir

ALU = mybir.AluOpType
ACT = mybir.ActivationFunctionType
AX_X = mybir.AxisListType.X
F32 = mybir.dt.float32
F32R = mybir.dt.float32r
BF16 = mybir.dt.bfloat16
U32 = mybir.dt.uint32

START = 1
FIRST = 16
P = 128
B, S, H = 8, 512, 512
NH, HD = 16, 32
E, TOPK, CAP, I = 64, 4, 64, 384
T = B * S
NT = S // P
KC = H // P
IC = I // P
NG = NH * HD // P
GH = NH // NG
PAIRS = E // 2 // B
assert PAIRS == NG
SCALE = HD ** -0.5
EPS = 1e-5
SPLIT = 3 * HD
SHIFT = SPLIT + 2
KOFF = (0, 512, 1024, 896)
PW = 1280


def three_products(nc, out, left, right, chunks):
    last = None
    terms = [(c, a, b) for c in chunks for a, b in ((0, 0), (0, 1), (1, 0))]
    for m, (c, a, b) in enumerate(terms):
        last = nc.tensor.matmul(out, left(a, c), right(b, c), start=(m == 0), stop=(m == len(terms) - 1))
    return last


def build(nc, d):
    with ExitStack() as whole:
        def sbw(name, shape, dt=F32):
            return whole.enter_context(nc.sbuf_tensor(name, shape, dt))

        ident = sbw("ident", [P, P])
        w_parts = [sbw(f"w_{'hl'[a]}", [P, 4, KC, H], F32R) for a in range(2)]
        stage_one(nc, d, ident, w_parts)
        stage_two(nc, d, ident, w_parts)


def stage_one(nc, d, ident, w_parts):
    with ExitStack() as ctx:
        def sb(name, shape, dt=F32):
            return ctx.enter_context(nc.sbuf_tensor(name, shape, dt))

        def sem(name):
            return ctx.enter_context(nc.semaphore(name))

        counts = []

        def count(name):
            counts.append(sem(name))
            return counts[-1]

        def banks(name, n):
            return [ctx.enter_context(nc.psum_tensor(f"{name}{j}", [P, 512], F32)) for j in range(n)]

        tp, gt, up, yb = banks("tp", 2), banks("gt", 2), banks("up", 2), banks("yb", 2)

        stage = sb("stage", [P, 2, KC * H])
        sg = [sb(f"sg_{a}", [P, KC, I], F32R) for a in "hl"]
        su = [sb(f"su_{a}", [P, KC, I], F32R) for a in "hl"]
        sd = [sb(f"sd_{a}", [P, IC, H], F32R) for a in "hl"]
        wr = [sb(f"wr_{a}", [P, KC, P], F32R) for a in "hl"]
        x_in = sb("x_in", [P, 2, NT, H])
        xn = sb("xn", [P, NT, H])
        xT = [sb(f"xT_{a}", [P, KC, S], F32R) for a in "hl"]
        h = sb("h", [P, 2, S])
        hT = [sb(f"hT_{a}", [P, IC, S], F32R) for a in "hl"]
        y_out = sb("y_out", [P, 2, H])
        stat = sb("stat", [P, NT, 6])
        mv = sb("mv", [P, NT, 2])
        veps = sb("veps", [P, NT])
        rstd = sb("rstd", [P, NT])
        neg_half = sb("neg_half", [P, NT])
        idle = sb("idle", [P, 1])
        pool_idle = sb("pool_idle", [P, 4])
        lgT = sb("lgT", [P, S])
        lg = sb("lg", [P, NT, E])
        top = sb("top", [P, NT, 8])
        top_i = sb("top_i", [P, NT, 8], U32)
        ex = sb("ex", [P, NT, TOPK])
        esum = sb("esum", [P, NT])
        wtok = sb("wtok", [P, NT, TOPK])
        idx_f = sb("idx_f", [P, NT * TOPK])
        iota_e = sb("iota_e", [P, E])
        onehot = sb("onehot", [P, NT * TOPK, E])
        prod = sb("prod", [P, NT * TOPK, E])
        chosen = sb("chosen", [P, NT, E], BF16)
        chosen_sum = sb("chosen_sum", [P, E])
        before = sb("before", [P, E])
        before_b = sb("before_b", [P, E], BF16)
        lower = sb("lower", [P, P])
        lower_b = sb("lower_b", [P, P], BF16)
        ones_b = sb("ones_b", [P, P], BF16)
        tok = sb("tok", [P, NT])
        spill = sb("spill", [P, NT * TOPK])
        place = sb("place", [P, NT * TOPK])
        fits = sb("fits", [P, NT * TOPK])
        row = sb("row", [P, NT * TOPK])
        row_u = sb("row_u", [P, 2, NT * TOPK], U32)
        entry = sb("entry", [P, 2, NT * TOPK, 2])

        const_in = sem("const_in")
        init_done = sem("init_done")
        w_loaded = [sem(f"w_loaded{j}") for j in range(2)]
        w_hi, w_lo = sem("w_hi"), sem("w_lo")
        wa_loaded, wa_hi, wa_lo = count("wa_loaded"), count("wa_hi"), count("wa_lo")
        stats = count("stats")
        x_loaded = [count(f"x_loaded{u}") for u in range(2)]
        x_free = [count(f"x_free{u}") for u in range(2)]
        dv = count("dv")
        var_ready, rstd_ready, pool_const = count("var_ready"), count("rstd_ready"), sem("pool_const")
        xn_ready, xn_stored = count("xn_ready"), count("xn_stored")
        tp_full, logits_read, rank_read = count("tp_full"), count("logits_read"), count("rank_read")
        xT_hi, xT_lo = count("xT_hi"), count("xT_lo")
        lgT_ready, ex_in, ex_ready = count("lgT_ready"), count("ex_in"), count("ex_ready")
        gu_full = count("gu_full")
        tanh_ready, h_ready, hT_hi, hT_lo = count("tanh_ready"), count("h_ready"), count("hT_hi"), count("hT_lo")
        y_full = count("y_full")
        y_ready, y_stored = count("y_ready"), [count(f"y_stored{u}") for u in range(2)]
        chosen_ready = count("chosen_ready")
        entry_ready, entry_done = count("entry_ready"), [sem(f"entry_done{u}") for u in range(2)]

        xv = d["x"].rearrange("(n t p) c -> n p t c", t=NT, p=P)
        xnv = d["xn_rows"][0:T, :].rearrange("(n t p) c -> n p t c", t=NT, p=P)
        ov = d["out"][0:T, :].rearrange("(n t p) c -> n t p c", t=NT, p=P)
        weights = [(d["wrT2"].rearrange("(k p) i -> p k i", p=P), wr, P),
                   (d["sh_gate"].rearrange("(k p) i -> p k i", p=P), sg, I),
                   (d["sh_up"].rearrange("(k p) i -> p k i", p=P), su, I),
                   (d["sh_down"].rearrange("(k p) i -> p k i", p=P), sd, H)]
        NW = len(weights)
        wTv = d["wT"].rearrange("j (k p) o -> j p k o", p=P)

        def staged(n):
            src, _, width = weights[n]
            k = src.shape[1]
            return stage[:, n % 2, 0:k * width].rearrange("p (k n) -> p k n", k=k)

        CONSTS = [(ident, "ident"), (iota_e, "iota_e"), (lower, "lower"), (tok, "tok0"), (spill, "spill0")]

        TP_LOGITS_T, TP_LOGITS, TP_RANK, TP_N = KC, KC + 1, KC + 2, KC + 3

        def tp_use(i, u, k):
            if k < KC:
                m = k if type(i) is int and i + u == 0 else TP_N * u + k - 1
            elif k == TP_RANK:
                m = TP_N * u + TP_N + KC - 1
            else:
                m = TP_N * u + k
            bank = m % 2
            if k == TP_RANK and type(i) is int and 2 * i + u == B - 1:
                m -= KC
            return tp[bank], START + 2 * TP_N * i + m + 1

        def tp_released(n, k, after=1):
            if k == TP_RANK and not after:
                return lgT_ready, START + n + 1
            read, value = [(lgT_ready, n), (logits_read, n), (xT_lo, KC * n + 1), (xT_lo, KC * n + 2),
                           (xT_lo, KC * n + KC), (rank_read, n), (xT_lo, KC * (n + 1) + 3)][k]
            return read, START + value

        def both(body, eng):
            with eng.Fori(0, B // 2 - 1) as i:
                for u in range(2):
                    body(i, u, 2)
            for u in range(2):
                body(B // 2 - 1, u, 1 - u)

        block = ctx.enter_context(nc.Block())

        @block.sync
        def _(sp):
            for s in counts:
                sp.sem_inc(s, START)
            for t, name in CONSTS:
                sp.dma_start(t[:], d[name]).then_inc(const_in, 16)
            sp.dma_start(d["out"][T:T + CAP, :], d["zeros"]).then_inc(init_done, 16)

            def load_x(i, u):
                sp.wait_ge(x_free[u], START + i)
                sp.dma_start(x_in[:, u], xv[bass.ds(2 * i + u, 1)].rearrange("o p t c -> p (o t) c"))\
                    .then_inc(x_loaded[u], 16)

            def store_xn(n):
                sp.wait_ge(xn_ready, START + n + 1)
                sp.dma_start(xnv[bass.ds(n, 1)].rearrange("o p t c -> p (o t) c"), xn[:]).then_inc(xn_stored, 16)

            load_x(0, 0)
            for n, (src, parts, width) in enumerate(weights):
                if n >= 2:
                    sp.wait_ge(w_hi, n - 1)
                    sp.wait_ge(w_lo, n - 1)
                sp.dma_start(staged(n), src).then_inc(w_loaded[n % 2], 16)
            load_x(0, 1)
            store_xn(0)
            sp.wait_ge(w_lo, NW)

            def sequence(i, u, after):
                n = 2 * i + u
                if u == 0:
                    sp.wait_ge(wa_lo, START + i)
                    sp.dma_start(stage[:, 0].rearrange("p (k n) -> p k n", k=KC),
                                 wTv[bass.ds(i, 1)].rearrange("o p k n -> p (o k) n")).then_inc(wa_loaded, 16)
                if after:
                    store_xn(n + 1)
                for t in range(NT):
                    sp.wait_ge(y_ready, START + NT * n + t + 1)
                    sp.dma_start(ov[bass.ds(n, 1), t].rearrange("o p c -> p (o c)"), y_out[:, t % 2])\
                        .then_inc(y_stored[t % 2], 16)
                if after == 2:
                    load_x(i + 1, u)

            both(sequence, sp)
            sp.wait_ge(init_done, 16)
            sp.wait_ge(xn_stored, START + 16 * B)
            for u in range(2):
                sp.wait_ge(y_stored[u], START + 16 * B * NT // 2)

        @block.gpsimd
        def _(pool):
            nc.gpsimd.memset(neg_half[:], -0.5).then_inc(pool_const, 1)
            nc.gpsimd.dma_start(d["slots"][0:E * CAP, :], d["slots0"]).then_inc(entry_done[0], FIRST)
            nc.gpsimd.dma_start(d["xn_rows"][T:T + CAP, :], d["zeros"]).then_inc(entry_done[1], FIRST)
            pool.wait_ge(pool_const, 1)
            for u in range(2):
                pool.wait_ge(entry_done[u], FIRST)

            def inverse_deviation(n):
                pool.wait_ge(var_ready, START + n + 1)
                nc.gpsimd.tensor_tensor(rstd[:], veps[:], neg_half[:], ALU.pow).then_inc(rstd_ready, 1)

            inverse_deviation(0)

            def sequence(i, u, after):
                n = 2 * i + u
                if after:
                    inverse_deviation(n + 1)
                pool.wait_ge(entry_ready, START + n + 1)
                cell = u if after == 2 else 2 + u
                nc.gpsimd.tensor_tensor(pool_idle[:, cell:cell + 1], neg_half[:, 0:1], neg_half[:, 1:2], ALU.add)
                for k in range(NT * TOPK):
                    nc.gpsimd.indirect_dma_start(
                        out=d["slots"], out_offset=bass.IndirectOffsetOnAxis(ap=row_u[:, u, k:k + 1], axis=0),
                        in_=entry[:, u, k, :], in_offset=None).then_inc(entry_done[u], 16)

            both(sequence, pool)
            for u in range(2):
                pool.wait_ge(entry_done[u], FIRST + 16 * NT * TOPK * B // 2)

        @block.scalar
        def _(act):
            def x_high(i, u):
                n = 2 * i + u
                act.wait_ge(gu_full, START + IC * n)
                for k in range(KC):
                    b, full = tp_use(i, u, k)
                    act.wait_ge(tp_full, full)
                    nc.scalar.activation(xT[0][:, k], b[:], ACT.Copy).then_inc(xT_hi, 1)

            for n, (src, parts, width) in enumerate(weights):
                act.wait_ge(w_loaded[n % 2], 16 * (n // 2 + 1))
                nc.scalar.activation(parts[0][:], staged(n), ACT.Copy).then_inc(w_hi, 1)
                if n == 1:
                    x_high(0, 0)

            def sequence(i, u, after):
                n = 2 * i + u
                b, full = tp_use(i, u, TP_LOGITS_T)
                act.wait_ge(tp_full, full)
                nc.scalar.activation(lgT[:], b[:], ACT.Copy).then_inc(lgT_ready, 1)
                for c in range(IC):
                    m = IC * u + c
                    act.wait_ge(gu_full, START + 2 * IC * i + m + 1)
                    act.wait_ge(hT_lo, START + 2 * IC * i + max(m - 1, 0))
                    nc.scalar.activation(h[:, m % 2], gt[m % 2][:], ACT.Tanh, scale=0.5).then_inc(tanh_ready, 1)
                    act.wait_ge(h_ready, START + 2 * IC * i + m + 1)
                    if c == 0:
                        act.wait_ge(y_full, START + NT * n)
                    nc.scalar.activation(hT[0][:, c], h[:, m % 2], ACT.Copy).then_inc(hT_hi, 1)
                    if c == 1:
                        act.wait_ge(ex_in, START + n + 1)
                        nc.scalar.activation(ex[:], ex[:], ACT.Exp).then_inc(ex_ready, 1)
                if after:
                    x_high(i + u, 1 - u)
                if u == 0:
                    act.wait_ge(wa_loaded, START + 16 * (i + 1))
                    nc.scalar.activation(w_parts[0][:, bass.ds(i, 1)].rearrange("p o k n -> p (o k n)"), stage[:, 0],
                                         ACT.Copy).then_inc(wa_hi, 1)

            both(sequence, act)

        @block.vector
        def _(dve):
            dve.wait_ge(const_in, 16 * len(CONSTS))
            nc.vector.memset(before[:], 0.0)
            nc.vector.memset(before_b[:], 0.0)
            nc.vector.memset(ones_b[:], 1.0)
            nc.vector.tensor_copy(lower_b[:], lower[:]).then_inc(chosen_ready, 1)
            def link(ins, sem, value):
                ins.then_inc(sem, 1)
                dve.wait_ge(sem, START + value)

            def apart():
                nc.vector.memset(idle[:], 0.0)

            def normalize(i, u):
                n = 2 * i + u
                dve.wait_ge(x_loaded[u], START + 16 * (i + 1))
                apart()
                for t in range(NT):
                    last = nc.vector.bn_stats(stat[:, t], x_in[:, u, t])
                link(last, stats, 2 * n + 1)
                apart()
                for t in range(NT):
                    last = nc.vector.bn_aggr(mv[:, t], stat[:, t])
                link(last, stats, 2 * n + 2)
                nc.vector.tensor_scalar(veps[:], mv[:, :, 1], EPS, None, ALU.add).then_inc(var_ready, 1)
                dve.wait_ge(xn_stored, START + 16 * n)
                dve.wait_ge(xT_lo, START + KC * n)
                dve.wait_ge(rstd_ready, START + n + 1)
                for t in range(NT):
                    last = nc.vector.tensor_scalar(xn[:, t], x_in[:, u, t], mv[:, t, 0:1], rstd[:, t:t + 1],
                                                   ALU.subtract, ALU.mult)
                last.then_inc(xn_ready, 1)

            def x_low(i, u, chunks=range(KC)):
                n = 2 * i + u
                for k in chunks:
                    b, full = tp_use(i, u, k)
                    dve.wait_ge(xT_hi, START + KC * n + k + 1)
                    nc.vector.tensor_tensor(xT[1][:, k], b[:], xT[0][:, k].bitcast(F32), ALU.subtract)\
                        .then_inc(xT_lo, 1)

            normalize(0, 0)
            for n, (src, parts, width) in enumerate(weights):
                dve.wait_ge(w_hi, n + 1)
                nc.vector.tensor_tensor(parts[1][:], staged(n), parts[0][:].bitcast(F32), ALU.subtract)\
                    .then_inc(w_lo, 1)
                if n == 1:
                    x_low(0, 0)
            CHAIN = 20
            straight = link

            def sequence(i, u, after):
                n = 2 * i + u
                links = [0]

                def link(ins):
                    links[0] += 1
                    straight(ins, dv, CHAIN * n + links[0])

                def gate(c):
                    m = IC * u + c
                    dve.wait_ge(tanh_ready, START + 2 * IC * i + m + 1)
                    hb = h[:, m % 2]
                    link(nc.vector.scalar_tensor_tensor(out=hb, in0=hb, scalar=1.0, in1=gt[m % 2][:],
                                                        op0=ALU.add, op1=ALU.mult))
                    nc.vector.scalar_tensor_tensor(out=hb, in0=hb, scalar=0.5, in1=up[m % 2][:],
                                                   op0=ALU.mult, op1=ALU.mult)\
                        .then_inc(h_ready, 1)
                    dve.wait_ge(hT_hi, START + 2 * IC * i + m + 1)
                    nc.vector.tensor_tensor(hT[1][:, c], hb, hT[0][:, c].bitcast(F32), ALU.subtract)\
                        .then_inc(hT_lo, 1)

                b, full = tp_use(i, u, TP_LOGITS)
                gate(0)
                dve.wait_ge(tp_full, full)
                link(nc.vector.tensor_copy(lg[:], b[:].rearrange("p (t e) -> p t e", t=NT)[:, :, 0:E]))
                apart()
                for t in range(NT):
                    last = nc.vector.max(top[:, t], lg[:, t])
                link(last)
                apart()
                for t in range(NT):
                    last = nc.vector.max_index(top_i[:, t], top[:, t], lg[:, t])
                last.then_inc(logits_read, 1)
                link(nc.vector.tensor_tensor(ex[:], top[:, :, 0:TOPK], top[:, :, 0:1].to_broadcast([P, NT, TOPK]),
                                             ALU.subtract))
                nc.vector.tensor_copy(idx_f[:].rearrange("p (t j) -> p t j", j=TOPK), top_i[:, :, 0:TOPK])\
                    .then_inc(ex_in, 1)
                dve.wait_ge(ex_in, START + n + 1)
                link(nc.vector.tensor_tensor(onehot[:], iota_e[:].unsqueeze(1).to_broadcast([P, NT * TOPK, E]),
                                             idx_f[:].unsqueeze(2).to_broadcast([P, NT * TOPK, E]), ALU.is_equal))
                oh = onehot[:].rearrange("p (t j) e -> p t j e", j=TOPK)
                pr = prod[:].rearrange("p (t j) e -> p t j e", j=TOPK)
                link(nc.vector.tensor_tensor(pr[:, :, 0:2], oh[:, :, 0:2], oh[:, :, 2:4], ALU.add))
                nc.vector.tensor_tensor(chosen[:], pr[:, :, 0], pr[:, :, 1], ALU.add).then_inc(chosen_ready, 1)
                gate(1)
                dve.wait_ge(ex_ready, START + n + 1)
                link(nc.vector.reduce_sum(esum[:], ex[:], AX_X))
                link(nc.vector.reciprocal(esum[:], esum[:]))
                dve.wait_ge(entry_done[u], FIRST + 16 * NT * TOPK * i)
                nc.vector.tensor_tensor(entry[:, u, :, 1].rearrange("p (t j) -> p t j", j=TOPK), ex[:],
                                        esum[:].unsqueeze(2).to_broadcast([P, NT, TOPK]), ALU.mult)
                link(nc.vector.tensor_copy(entry[:, u, :, 0].rearrange("p (t j) -> p t j", j=TOPK),
                                           tok[:].unsqueeze(2).to_broadcast([P, NT, TOPK])))
                if after:
                    normalize(i + u, 1 - u)
                gate(2)
                for t in range(NT):
                    if after and t % 2 == 0:
                        x_low(i + u, 1 - u, (t, t + 1))
                    yu = t % 2
                    dve.wait_ge(y_full, START + NT * n + t + 1)
                    dve.wait_ge(y_stored[yu], START + 16 * (2 * n + t // 2))
                    nc.vector.tensor_tensor(y_out[:, yu], yb[yu][:], x_in[:, u, t], ALU.add)\
                        .then_inc(y_ready, 1)
                b, full = tp_use(i, u, TP_RANK)
                dve.wait_ge(tp_full, full)
                rank = b[:, 0:NT * E].rearrange("p (t e) -> p t e", e=E)
                nc.vector.tensor_tensor(pr, oh, rank.unsqueeze(2).to_broadcast([P, NT, TOPK, E]), ALU.mult)\
                    .then_inc(rank_read, 1)
                dve.wait_ge(rank_read, START + n + 1)
                link(nc.vector.reduce_sum(place[:], prod[:], AX_X))
                nc.vector.tensor_scalar(fits[:], place[:], float(CAP), None, ALU.is_lt)
                link(nc.vector.scalar_tensor_tensor(out=row[:], in0=idx_f[:], scalar=float(CAP), in1=place[:],
                                                    op0=ALU.mult, op1=ALU.add))
                link(nc.vector.tensor_tensor(row[:], row[:], spill[:], ALU.subtract))
                link(nc.vector.tensor_tensor(row[:], row[:], fits[:], ALU.mult))
                link(nc.vector.tensor_tensor(row[:], row[:], spill[:], ALU.add))
                nc.vector.tensor_copy(row_u[:, u], row[:]).then_inc(entry_ready, 1)
                nc.vector.tensor_scalar(tok[:], tok[:], float(S), None, ALU.add).then_inc(x_free[u], 1)
                nc.vector.tensor_scalar(spill[:], spill[:], float(S * TOPK), None, ALU.add)
                link(nc.vector.tensor_tensor(pr[:, 0:2, 0], chosen[:, 0:2], chosen[:, 2:4], ALU.add))
                link(nc.vector.tensor_tensor(chosen_sum[:], pr[:, 0, 0], pr[:, 1, 0], ALU.add))
                link(nc.vector.tensor_tensor(before[:], before[:], chosen_sum[:], ALU.add))
                link(nc.vector.tensor_copy(before_b[:], before[:]))
                if u == 0:
                    dve.wait_ge(wa_hi, START + i + 1)
                    wa = [w[:, bass.ds(i, 1)].rearrange("p o k n -> p (o k n)") for w in w_parts]
                    nc.vector.tensor_tensor(wa[1], stage[:, 0], wa[0].bitcast(F32), ALU.subtract).then_inc(wa_lo, 1)
                assert links[0] == CHAIN, links[0]

            both(sequence, dve)

        @block.tensor
        def _(pe):
            pe.wait_ge(const_in, 16 * len(CONSTS))
            pe.wait_ge(chosen_ready, START + 1)

            def turn_x(i, u, chunks=range(KC)):
                n = 2 * i + u
                pe.wait_ge(xn_ready, START + n + 1)
                for k in chunks:
                    b, _ = tp_use(i, u, k)
                    pe.wait_ge(*tp_released(n, k))
                    for t in range(NT):
                        last = nc.tensor.transpose(b[:, t * P:(t + 1) * P], xn[:, t, k * P:(k + 1) * P], ident[:])
                    last.then_inc(tp_full, 1)

            turn_x(0, 0)

            def sequence(i, u, after):
                n = 2 * i + u
                pe.wait_ge(xT_lo, START + KC * (n + 1))
                b, _ = tp_use(i, u, TP_LOGITS_T)
                pe.wait_ge(w_lo, 1)
                pe.wait_ge(*tp_released(n, TP_LOGITS_T))
                three_products(nc, b[:], lambda a, k: wr[a][:, k], lambda a, k: xT[a][:, k], range(KC))\
                    .then_inc(tp_full, 1)
                for c in range(IC):
                    m = IC * u + c
                    pe.wait_ge(w_lo, 3)
                    pe.wait_ge(h_ready, START + 2 * IC * i + max(m - 1, 0))
                    for w, bank in ((sg, gt), (su, up)):
                        last = three_products(nc, bank[m % 2][:], lambda a, k: w[a][:, k, c * P:(c + 1) * P],
                                              lambda a, k: xT[a][:, k], range(KC))
                    last.then_inc(gu_full, 1)
                    if c == 0:
                        b, _ = tp_use(i, u, TP_LOGITS)
                        pe.wait_ge(lgT_ready, START + n + 1)
                        pe.wait_ge(*tp_released(n, TP_LOGITS))
                        for t in range(NT):
                            last = nc.tensor.transpose(b[:, t * P:(t + 1) * P], lgT[:, t * P:(t + 1) * P], ident[:])
                        last.then_inc(tp_full, 1)
                if after:
                    turn_x(i + u, 1 - u, (0, 1))

                def down(t, chunks):
                    yu = t % 2
                    for m, (c, p, q) in enumerate((c, p, q) for c in chunks for p, q in ((0, 0), (0, 1), (1, 0))):
                        last = nc.tensor.matmul(yb[yu][:], hT[p][:, c, t * P:(t + 1) * P], sd[q][:, c],
                                                start=(c == 0 and m == 0), stop=(c == IC - 1 and m % 3 == 2))
                    if chunks[-1] == IC - 1:
                        last.then_inc(y_full, 1)

                pe.wait_ge(w_lo, NW)
                pe.wait_ge(y_ready, START + NT * n)
                pe.wait_ge(hT_lo, START + IC * (n + 1) - 1)
                down(0, range(IC - 1))
                down(1, range(IC - 1))
                pe.wait_ge(hT_lo, START + IC * (n + 1))
                down(0, [IC - 1])
                down(1, [IC - 1])
                pe.wait_ge(y_ready, START + NT * n + 1)
                down(2, range(IC))
                if after:
                    turn_x(i + u, 1 - u, (2, 3))
                pe.wait_ge(y_ready, START + NT * n + 2)
                down(3, range(IC))
                b, _ = tp_use(i, u, TP_RANK)
                pe.wait_ge(*tp_released(n, TP_RANK, after))
                pe.wait_ge(chosen_ready, START + n + 2)
                rank = b[:, 0:NT * E]
                nc.tensor.matmul(rank, lower_b[:], chosen[:].rearrange("p t e -> p (t e)"), start=True, stop=False)
                for t in range(NT - 1):
                    later = NT - 1 - t
                    nc.tensor.matmul(b[:, (t + 1) * E:NT * E], ones_b[:],
                                     chosen[:, t:t + 1].to_broadcast([P, later, E]), start=False, stop=False)
                nc.tensor.matmul(rank, ones_b[:], before_b[:].unsqueeze(1).to_broadcast([P, NT, E]),
                                 start=False, stop=True).then_inc(tp_full, 1)

            both(sequence, pe)


def stage_two(nc, d, ident, w_parts):
    with ExitStack() as ctx:
        def sb(name, shape, dt=F32):
            return ctx.enter_context(nc.sbuf_tensor(name, shape, dt))

        def sem(name):
            return ctx.enter_context(nc.semaphore(name))

        counts = []

        def count(name):
            counts.append(sem(name))
            return counts[-1]

        def bank(name):
            return ctx.enter_context(nc.psum_tensor(name, [P, 512], F32))

        ring = [bank(f"ring{j}") for j in range(4)]
        o_bank, sum_bank = bank("o_bank"), bank("sum_bank")
        ea, eb = bank("ea"), bank("eb")

        xo = [sb(f"xo_{a}", [P, KC, S], F32R) for a in "hl"]
        qk = sb("qk", [P, 2, NT, H])
        v = sb("v", [P, NT, H])
        t1 = sb("t1", [P, H])
        t2 = sb("t2", [P, H])
        parts = sb("parts", [P, 2, NT, GH, SPLIT], F32R)
        stacks = [sb(f"stack_{a}", [P, GH, S], F32R) for a in "qk"]
        prob = sb("prob", [P, GH, PW])
        wo_out = sb("wo_out", [P, NT, H])
        wgu = sb("wgu", [P, 2, 2, KC, I])
        wdn = sb("wdn", [P, 2, IC, H])
        xe = sb("xe", [P, H])
        xeT = sb("xeT", [P, KC, P])
        he = sb("he", [P, I])
        heT = sb("heT", [P, IC, P])
        ye = sb("ye", [P, H])
        cos, sin = sb("cos", [P, NT, HD]), sb("sin", [P, NT, HD])
        mask = sb("mask", [P, S], BF16)
        ones = sb("ones", [P, HD])
        peak = sb("peak", [P, NT, GH])
        shift = sb("shift", [P, NT, GH, HD], F32R)
        table = sb("table", [P, E // 2, 2])
        table_s = sb("table_s", [CAP, E, 2])
        row_g = sb("row_g", [P, E // 2], U32)
        row_s = sb("row_s", [CAP, E], U32)
        now_g = sb("now_g", [P, 1], U32)
        now_s = sb("now_s", [CAP, 2], U32)
        pool_zero = sb("pool_zero", [P, 2])
        pool_idle = sb("pool_idle2", [P, 48])
        idle = sb("idle2", [P, 10 * NG])

        const_in, const_set, pool_const = sem("const_in2"), sem("const_set"), sem("pool_const2")
        table_in, table_ready = sem("table_in"), sem("table_ready")
        x_in = count("x_in2")
        ring_full = count("ring_full")
        xo_hi, xo_lo = count("xo_hi"), count("xo_lo")
        rope_read, qk_ready, v_ready = count("rope_read"), count("qk_ready"), count("v_ready")
        part_hi, part_dup, part_lo = count("part_hi"), count("part_dup"), count("part_lo")
        q_ready, k_ready = count("q_ready"), count("k_ready")
        s_read, shift_hi, shift_lo, shift_in = count("s_read"), count("shift_hi"), count("shift_lo"), count("shift_in")
        exp_done, masked, pv_done = count("exp_done"), count("masked"), count("pv_done")
        o_inv, o_ready, o_hi, o_lo = count("o_inv"), count("o_ready"), count("o_hi"), count("o_lo")
        wo_ready = count("wo_ready")
        gu_in, dn_in = count("gu_in"), count("dn_in")
        xe_in, xeT_full, xeT_ready = sem("xe_in"), count("xeT_full"), count("xeT_ready")
        gu_full, tanh_ready, gated, he_ready = count("gu_full2"), count("tanh_ready2"), count("gated"), count("he_ready")
        heT_full, heT_ready, ye_full, ye_ready = count("heT_full"), count("heT_ready"), count("ye_full"), count("ye_ready")
        now_set, added = count("now_set"), sem("added")

        def s_pieces(width):
            full, three, two, one = (sorted(range(NT), key=lambda t: -width[t]))
            out = []
            for hh in range(2):
                out.append([(hh, full, 0, width[full])])
                out.append([(hh, three, 0, width[three]), (hh, one, width[three], width[one])])
            out.append([(hh, two, hh * width[two], width[two]) for hh in range(2)])
            return out

        S_PIECES = [(pair, piece) for pair in range(2) for piece in s_pieces([P * (t + 1) for t in range(NT)])]
        S_N = len(S_PIECES)
        S_PARTS = (range(0, 4), range(4, 7), range(7, S_N))
        T_PIECES = s_pieces([P * (NT - t) for t in range(NT)])
        EXPS = sum(len(x) for x in T_PIECES)

        uses = [(("x", k), xo_lo, k + 1) for k in range(KC)]
        uses += [(("qk", t, j), rope_read, 2 * t + j + 1) for t in range(NT) for j in range(2)]

        def v_uses(*tiles):
            return [(("v", t), v_ready, t + 1) for t in tiles]

        def stack_uses(g):
            return [(("stack", g, h, j), (q_ready, k_ready)[j], GH * g + h + 1) for h in range(GH) for j in range(2)]

        def s_uses(g, part):
            return [(("s", g, m), s_read, S_N * g + m + 1) for m in S_PARTS[part]]

        uses += v_uses(0, 1) + stack_uses(0)
        for g in range(NG):
            uses += s_uses(g, 0) + (v_uses(2) if g == 0 else []) + s_uses(g, 1) + (v_uses(3) if g == 0 else [])
            uses += s_uses(g, 2)
            uses += [(("shift", g), shift_in, GH * (g + 1))]
            for pair in range(2):
                done = EXPS * (2 * g + pair)
                for m in range(5):
                    done += len(T_PIECES[m])
                    uses += [(("t", g, pair, m), exp_done, done)]
            if g < NG - 1:
                uses += stack_uses(g + 1)
        uses += [(("wo", t), wo_ready, t + 1) for t in range(NT)]
        RING_N = len(uses)
        number = {name: m for m, (name, _, _) in enumerate(uses)}
        assert RING_N % 4 == 0
        each = {xo_lo: KC, rope_read: 2 * NT, v_ready: NT, q_ready: NH, k_ready: NH, s_read: S_N * NG,
                shift_in: GH * NG, exp_done: EXPS * 2 * NG, wo_ready: NT}

        def bank_of(*name):
            return ring[number[name] % 4]

        def full(i, *name):
            return ring_full, START + RING_N * i + number[name] + 1

        def released(i, *name):
            m = number[name]
            if m < 4:
                return wo_ready, START + NT * i
            _, s, value = uses[m - 4]
            return s, START + each[s] * i + value

        ADDS = 2 * PAIRS + 1

        xnv = d["xn_rows"][0:T, :].rearrange("(n t p) c -> n p t c", t=NT, p=P)
        ov = d["out"][0:T, :].rearrange("(n t p) c -> n p t c", t=NT, p=P)
        gv = [d[n].rearrange("e (k p) i -> e p k i", p=P) for n in ("w_gate", "w_up")]
        dv_ = d["w_down"].rearrange("e (k p) i -> e p k i", p=P)

        def all_sequences(body, eng):
            with eng.Fori(0, B - 1) as i:
                body(i, True)
            body(B - 1, False)

        block = ctx.enter_context(nc.Block())

        @block.sync
        def _(sp):
            for s in counts:
                sp.sem_inc(s, START)
            sp.dma_start(cos[:], d["cos"]).then_inc(const_in, 16)
            sp.dma_start(sin[:], d["sin"]).then_inc(const_in, 16)
            lists = d["slots"][0:E * CAP, :]
            sp.dma_start(table[:], lists.rearrange("(q p) c -> p q c", p=P)).then_inc(table_in, 16)
            sp.dma_start(table_s[:], lists.rearrange("(e p) c -> p e c", p=CAP)).then_inc(table_in, 16)

            def load_x(n):
                sp.dma_start(qk[:, 0], xnv[bass.ds(n, 1)].rearrange("o p t c -> p (o t) c")).then_inc(x_in, 16)

            def gate_up(i, g):
                sp.wait_ge(gu_full, START + PAIRS * i + g)
                for ab in range(2):
                    for w in range(2):
                        sp.dma_start(wgu[:, w, ab], gv[w][bass.ds(i * 2 * PAIRS + (2 * g + ab), 1)]
                                     .rearrange("e p k i -> p (e k) i")).then_inc(gu_in, 16)

            def down(i, g):
                sp.wait_ge(ye_full, START + PAIRS * i + g)
                for ab in range(2):
                    sp.dma_start(wdn[:, ab], dv_[bass.ds(i * 2 * PAIRS + (2 * g + ab), 1)]
                                 .rearrange("e p k i -> p (e k) i")).then_inc(dn_in, 16)

            load_x(0)
            gate_up(0, 0)
            down(0, 0)

            def sequence(i, more):
                for g in range(1, PAIRS):
                    gate_up(i, g)
                    down(i, g)
                if more:
                    gate_up(i, PAIRS)
                    sp.wait_ge(part_lo, START + 2 * NG * (i + 1))
                    load_x(i + 1)
                    down(i, PAIRS)

            all_sequences(sequence, sp)

        @block.gpsimd
        def _(pool):
            nc.gpsimd.memset(pool_zero[:], 0.0).then_inc(pool_const, 1)
            pool.wait_ge(pool_const, 1)
            nc.gpsimd.dma_start(t1[:], d["mask"]).then_inc(added, FIRST)
            pool.wait_ge(table_ready, 1)

            def take_wait():
                n = next(pool_cells)
                nc.gpsimd.tensor_tensor(pool_idle[:, n:n + 1], pool_zero[:, 0:1], pool_zero[:, 1:2], ALU.add)

            pool_cells = iter(range(pool_idle.shape[1]))
            NOW = 2 * PAIRS
            now_count = iter((1, 2))

            def gather(i, g):
                pool.wait_ge(xeT_full, START + PAIRS * i + g)
                take_wait()
                nc.gpsimd.tensor_copy(now_g[:], row_g[:, bass.ds(i * PAIRS + g, 1)]).then_inc(now_set, 1)
                pool.wait_ge(now_set, START + NOW * i + next(now_count))
                take_wait()
                nc.gpsimd.indirect_dma_start(
                    out=xe[:], out_offset=None, in_=d["xn_rows"],
                    in_offset=bass.IndirectOffsetOnAxis(ap=now_g[:], axis=0)).then_inc(xe_in, 16)

            gather(0, 0)
            gather(0, 1)

            def sequence(i, more):
                nonlocal pool_cells, now_count
                pool_cells = iter(range(4, pool_idle.shape[1]))
                now_count = iter(range(3, NOW + 3))

                def scatter(g):
                    pool.wait_ge(ye_ready, START + PAIRS * i + g + 1)
                    pool.wait_ge(added, FIRST + 16 * (ADDS * i + 2 * g))
                    take_wait()
                    nc.gpsimd.tensor_copy(now_s[:], row_s[:, bass.ds((i * PAIRS + g) * 2, 2)]).then_inc(now_set, 1)
                    pool.wait_ge(now_set, START + NOW * i + next(now_count))
                    take_wait()
                    add_expert(g, 0)

                def add_expert(g, ab):
                    if ab:
                        pool.wait_ge(added, FIRST + 16 * (ADDS * i + 2 * g + 1))
                        take_wait()
                    nc.gpsimd.indirect_dma_start(
                        out=d["out"], out_offset=bass.IndirectOffsetOnAxis(ap=now_s[:, ab:ab + 1], axis=0),
                        in_=ye[ab * CAP:(ab + 1) * CAP, :], in_offset=None,
                        compute_op=ALU.add).then_inc(added, 16)

                def duplicate(g):
                    for j in range(2):
                        pool.wait_ge(part_hi, START + 2 * NG * i + 2 * g + j + 1)
                        take_wait()
                        to = parts[:, j, :, :, HD * (1 + j):HD * (2 + j)]
                        nc.gpsimd.tensor_copy(to, parts[:, j, :, :, 0:HD].bitcast(F32)).then_inc(part_dup, 1)

                def causal(g, pair):
                    pool.wait_ge(exp_done, START + EXPS * (2 * NG * i + 2 * g + pair + 1))
                    take_wait()
                    for h in (2 * pair, 2 * pair + 1):
                        for view in (prob[:, h, 0:1024].rearrange("p (a b) -> p a b", a=2)[:, :, 0:P],
                                     prob[:, h, 896:1152].rearrange("p (a b) -> p a b", a=2)):
                            nc.gpsimd.affine_select(out=view, in_=view, compare_op=ALU.is_ge, fill=0.0, base=0,
                                                    pattern=[[0, 2], [1, P]], channel_multiplier=-1)\
                                .then_inc(masked, 1)

                scatter(0)
                add_expert(0, 1)
                duplicate(0)
                for g in range(NG):
                    if g + 2 < PAIRS or more:
                        gather(i, g + 2)
                    if g:
                        scatter(g)
                    causal(g, 0)
                    if g < NG - 1:
                        duplicate(g + 1)
                    if g and g < NG - 1:
                        add_expert(g, 1)
                    causal(g, 1)
                add_expert(NG - 1, 1)
                pool.wait_ge(wo_ready, START + NT * (i + 1))
                pool.wait_ge(added, FIRST + 16 * (ADDS * i + 2 * PAIRS))
                take_wait()
                nc.gpsimd.dma_start(ov[bass.ds(i, 1)].rearrange("o p t c -> p (o t) c"), wo_out[:],
                                    accum_op=ALU.add).then_inc(added, 16)

            all_sequences(sequence, pool)
            pool.wait_ge(added, FIRST + 16 * ADDS * B)

        @block.scalar
        def _(act):
            def expert_rows(i, g):
                act.wait_ge(xeT_full, START + PAIRS * i + g + 1)
                nc.scalar.activation(xeT[:].rearrange("p k n -> p (k n)"), ea[:], ACT.Copy).then_inc(xeT_ready, 1)

            def expert_tanh(i, g):
                act.wait_ge(gu_full, START + PAIRS * i + g + 1)
                act.wait_ge(heT_full, START + PAIRS * i + g)
                nc.scalar.activation(he[:], ea[:, 0:I], ACT.Tanh, scale=0.5).then_inc(tanh_ready, 1)

            def expert_turned(i, g):
                act.wait_ge(heT_full, START + PAIRS * i + g + 1)
                nc.scalar.activation(heT[:].rearrange("p k n -> p (k n)"), ea[:, 0:I], ACT.Copy)\
                    .then_inc(heT_ready, 1)

            expert_rows(0, 0)
            expert_tanh(0, 0)
            expert_turned(0, 0)

            def sequence(i, more):
                def split(g):
                    for j in range(2):
                        act.wait_ge(qk_ready, START + 2 * NT * (i + 1))
                        if g:
                            act.wait_ge(*full(i, "stack", g - 1, GH - 1, j))
                        else:
                            act.wait_ge(*full(i, "x", KC - 1))
                        nc.scalar.activation(parts[:, j, :, :, 0:HD],
                                             qk[:, j, :, g * P:(g + 1) * P].rearrange("p t (h e) -> p t h e", e=HD),
                                             ACT.Copy).then_inc(part_hi, 1)

                def stack(g):
                    for h in range(GH):
                        act.wait_ge(*full(i, "stack", g, h, 0))
                        nc.scalar.activation(stacks[0][0:SPLIT, h], bank_of("stack", g, h, 0)[0:SPLIT, :],
                                             ACT.Copy).then_inc(q_ready, 1)

                def exps(g, pair):
                    if pair == 0:
                        act.wait_ge(pv_done, START + NG * i + g)
                    for m, piece in enumerate(T_PIECES):
                        act.wait_ge(*full(i, "t", g, pair, m))
                        for hh, t, col, width in piece:
                            nc.scalar.activation(prob[:, 2 * pair + hh, KOFF[t]:KOFF[t] + width],
                                                 bank_of("t", g, pair, m)[:, col:col + width], ACT.Exp,
                                                 scale=SCALE).then_inc(exp_done, 1)

                def heads_out(g):
                    act.wait_ge(o_ready, START + NG * i + g + 1)
                    nc.scalar.activation(xo[0][:, g], t2[:], ACT.Copy).then_inc(o_hi, 1)

                def value(t):
                    act.wait_ge(*full(i, "v", t))
                    nc.scalar.activation(v[:, t], bank_of("v", t)[:], ACT.Copy).then_inc(v_ready, 1)

                for k in range(KC):
                    act.wait_ge(*full(i, "x", k))
                    nc.scalar.activation(xo[0][:, k], bank_of("x", k)[:], ACT.Copy).then_inc(xo_hi, 1)
                act.wait_ge(pv_done, START + NG * i)
                value(0)
                split(0)
                value(1)
                stack(0)
                value(2)
                value(3)
                for g in range(NG):
                    next_pair = g + 1 < PAIRS or more
                    if next_pair:
                        expert_rows(i, g + 1)
                    act.wait_ge(*full(i, "shift", g))
                    for h in range(GH):
                        nc.scalar.activation(stacks[0][SPLIT:SHIFT, h], bank_of("shift", g)[HD * h:HD * h + 2, :],
                                             ACT.Copy).then_inc(shift_in, 1)
                    exps(g, 0)
                    if g:
                        heads_out(g - 1)
                    if g < NG - 1:
                        split(g + 1)
                    if next_pair:
                        expert_tanh(i, g + 1)
                    exps(g, 1)
                    if g < NG - 1:
                        stack(g + 1)
                    if next_pair:
                        expert_turned(i, g + 1)
                heads_out(NG - 1)
                act.wait_ge(added, FIRST + 16 * ADDS * i)
                for t in range(NT):
                    act.wait_ge(*full(i, "wo", t))
                    nc.scalar.activation(wo_out[:, t], bank_of("wo", t)[:], ACT.Copy).then_inc(wo_ready, 1)

            all_sequences(sequence, act)

        @block.vector
        def _(dve):
            dve.wait_ge(table_in, 32)
            nc.vector.tensor_copy(row_g[:], table[:, :, 0])
            nc.vector.tensor_copy(row_s[:], table_s[:, :, 0]).then_inc(table_ready, 1)
            dve.wait_ge(const_in, 2 * 16)
            dve.wait_ge(added, FIRST)
            nc.vector.tensor_copy(mask[:], t1[:])
            nc.vector.memset(ones[:], 1.0)
            nc.vector.memset(shift[:].bitcast(F32), 0.0)
            nc.vector.memset(stacks[1][SPLIT:SHIFT].bitcast(F32), 1.0).then_inc(const_set, 1)
            dve.wait_ge(const_set, 1)

            def expert_gate(i, g):
                n = PAIRS * i + g + 1
                dve.wait_ge(tanh_ready, START + n)
                nc.vector.scalar_tensor_tensor(out=he[:], in0=he[:], scalar=1.0, in1=ea[:, 0:I],
                                               op0=ALU.add, op1=ALU.mult).then_inc(gated, 1)
                dve.wait_ge(gated, START + n)
                nc.vector.scalar_tensor_tensor(out=he[:], in0=he[:], scalar=0.5, in1=eb[:, 0:I],
                                               op0=ALU.mult, op1=ALU.mult).then_inc(he_ready, 1)

            expert_gate(0, 0)

            def sequence(i, more):
                def split(g):
                    for j in range(2):
                        dve.wait_ge(part_hi, START + 2 * NG * i + 2 * g + j + 1)
                        nc.vector.tensor_tensor(parts[:, j, :, :, HD * (2 - j):HD * (3 - j)],
                                                qk[:, j, :, g * P:(g + 1) * P].rearrange("p t (h e) -> p t h e", e=HD),
                                                parts[:, j, :, :, 0:HD].bitcast(F32), ALU.subtract)\
                            .then_inc(part_lo, 1)

                def stack(g):
                    for h in range(GH):
                        dve.wait_ge(*full(i, "stack", g, h, 1))
                        nc.vector.tensor_copy(stacks[1][0:SPLIT, h], bank_of("stack", g, h, 1)[0:SPLIT, :])\
                            .then_inc(k_ready, 1)

                def peaks(g):
                    for m, (pair, piece) in enumerate(S_PIECES):
                        dve.wait_ge(*full(i, "s", g, m))
                        nc.vector.memset(idle[:, S_N * g + m:S_N * g + m + 1], 0.0)
                        for hh, t, col, width in piece:
                            part = bank_of("s", g, m)[:, col:col + width]
                            last = nc.vector.tensor_tensor_reduce(
                                out=part, in0=part, in1=mask[:, S - width:S], scale=1.0, scalar=-3e38,
                                op0=ALU.add, op1=ALU.max, accum_out=peak[:, t, 2 * pair + hh:2 * pair + hh + 1])
                        last.then_inc(s_read, 1)

                def heads_out(g):
                    dve.wait_ge(pv_done, START + NG * i + g + 1)
                    nc.vector.reciprocal(t1[:], sum_bank[:]).then_inc(o_inv, 1)
                    dve.wait_ge(o_inv, START + NG * i + g + 1)
                    nc.vector.tensor_tensor(t2[:], o_bank[:], t1[:], ALU.mult).then_inc(o_ready, 1)
                    dve.wait_ge(o_hi, START + NG * i + g + 1)
                    nc.vector.tensor_tensor(xo[1][:, g], t2[:], xo[0][:, g].bitcast(F32), ALU.subtract)\
                        .then_inc(o_lo, 1)

                def expert_out(g):
                    dve.wait_ge(ye_full, START + PAIRS * i + g + 1)
                    dve.wait_ge(added, FIRST + 16 * (ADDS * i + 2 * g))
                    nc.vector.tensor_scalar(ye[:], eb[:], table[:, bass.ds(i * PAIRS + g, 1), 1], None, ALU.mult)\
                        .then_inc(ye_ready, 1)

                for k in range(KC):
                    dve.wait_ge(xo_hi, START + KC * i + k + 1)
                    nc.vector.tensor_tensor(xo[1][:, k], bank_of("x", k)[:], xo[0][:, k].bitcast(F32), ALU.subtract)\
                        .then_inc(xo_lo, 1)
                for t in range(NT):
                    for j in range(2):
                        n = 2 * NT * i + 2 * t + j + 1
                        dve.wait_ge(*full(i, "qk", t, j))
                        dve.wait_ge(qk_ready, START + n - 1)
                        b = bank_of("qk", t, j)[:].rearrange("p (h e) -> p h e", e=HD)
                        a1, a2 = (x[:].rearrange("p (h e) -> p h e", e=HD) for x in (t1, t2))
                        nc.vector.tensor_tensor(a1, b, cos[:, t:t + 1, :].to_broadcast([P, NH, HD]), ALU.mult)
                        nc.vector.tensor_tensor(a2[:, :, 0:HD // 2], b[:, :, HD // 2:HD],
                                                sin[:, t:t + 1, 0:HD // 2].to_broadcast([P, NH, HD // 2]), ALU.mult)
                        nc.vector.tensor_tensor(a2[:, :, HD // 2:HD], b[:, :, 0:HD // 2],
                                                sin[:, t:t + 1, HD // 2:HD].to_broadcast([P, NH, HD // 2]), ALU.mult)\
                            .then_inc(rope_read, 1)
                        dve.wait_ge(rope_read, START + n)
                        nc.vector.tensor_tensor(qk[:, j, t], t1[:], t2[:], ALU.add).then_inc(qk_ready, 1)
                    if t == 1:
                        expert_out(0)
                split(0)
                stack(0)
                for g in range(NG):
                    peaks(g)
                    n = NG * i + g + 1
                    dve.wait_ge(s_read, START + S_N * n)
                    dve.wait_ge(*full(i, "stack", g, GH - 1, 1))
                    nc.vector.tensor_scalar(shift[:, :, :, 0], peak[:], -1.0, None, ALU.mult).then_inc(shift_hi, 1)
                    dve.wait_ge(shift_hi, START + n)
                    nc.vector.scalar_tensor_tensor(out=shift[:, :, :, 1], in0=peak[:], scalar=-1.0,
                                                   in1=shift[:, :, :, 0].bitcast(F32), op0=ALU.mult,
                                                   op1=ALU.subtract).then_inc(shift_lo, 1)
                    if g:
                        expert_out(g)
                        heads_out(g - 1)
                    if g < NG - 1:
                        split(g + 1)
                    if g + 1 < PAIRS or more:
                        expert_gate(i, g + 1)
                    if g < NG - 1:
                        stack(g + 1)
                heads_out(NG - 1)

            all_sequences(sequence, dve)

        @block.tensor
        def _(pe):
            pe.wait_ge(const_set, 1)

            def expert_rows(i, g):
                pe.wait_ge(xe_in, 16 * (PAIRS * i + g + 1))
                pe.wait_ge(heT_ready, START + PAIRS * i + g)
                for k in range(KC):
                    last = nc.tensor.transpose(ea[:, k * P:(k + 1) * P], xe[:, k * P:(k + 1) * P], ident[:])
                last.then_inc(xeT_full, 1)

            def expert_gate_up(i, g):
                pe.wait_ge(xeT_ready, START + PAIRS * i + g + 1)
                pe.wait_ge(ye_ready, START + PAIRS * i + g)
                pe.wait_ge(gu_in, START + 64 * (PAIRS * i + g + 1))
                for k in range(KC):
                    for w, b in ((0, ea), (1, eb)):
                        for ab in range(2):
                            last = nc.tensor.matmul(b[ab * CAP:(ab + 1) * CAP, 0:I],
                                                    xeT[:, k, ab * CAP:(ab + 1) * CAP], wgu[:, w, ab, k],
                                                    start=(k == 0), stop=(k == KC - 1), skip_group_check=True)
                last.then_inc(gu_full, 1)

            def expert_turn(i, g):
                pe.wait_ge(he_ready, START + PAIRS * i + g + 1)
                for c in range(IC):
                    last = nc.tensor.transpose(ea[:, c * P:(c + 1) * P], he[:, c * P:(c + 1) * P], ident[:])
                last.then_inc(heT_full, 1)

            expert_rows(0, 0)
            expert_gate_up(0, 0)
            expert_turn(0, 0)

            def sequence(i, more):
                def acquire(*name):
                    pe.wait_ge(*released(i, *name))
                    return bank_of(*name)

                def stack(g):
                    for h in range(GH):
                        for j in range(2):
                            pe.wait_ge(part_dup, START + 2 * NG * i + 2 * g + j + 1)
                            pe.wait_ge(part_lo, START + 2 * NG * i + 2 * g + j + 1)
                            b = acquire("stack", g, h, j)
                            for t in range(NT):
                                last = nc.tensor.transpose(b[0:SPLIT, t * P:(t + 1) * P],
                                                           parts[:, j, t, h].bitcast(F32), ident[:])
                            last.then_inc(ring_full, 1)

                def scores(g, part):
                    if part == 0:
                        pe.wait_ge(q_ready, START + GH * (NG * i + g + 1))
                        pe.wait_ge(k_ready, START + GH * (NG * i + g + 1))
                    for m in S_PARTS[part]:
                        pair, piece = S_PIECES[m]
                        b = acquire("s", g, m)
                        for hh, t, col, width in piece:
                            h = 2 * pair + hh
                            last = nc.tensor.matmul(b[:, col:col + width], stacks[0][0:SPLIT, h, t * P:(t + 1) * P],
                                                    stacks[1][0:SPLIT, h, 0:width], start=True, stop=True)
                        last.then_inc(ring_full, 1)

                def scores_t(g, pair):
                    for m, piece in enumerate(T_PIECES):
                        b = acquire("t", g, pair, m)
                        if pair == 0 and m == 0:
                            pe.wait_ge(shift_in, START + GH * (NG * i + g + 1))
                        for hh, t, col, width in piece:
                            h = 2 * pair + hh
                            last = nc.tensor.matmul(b[:, col:col + width], stacks[1][0:SHIFT, h, t * P:(t + 1) * P],
                                                    stacks[0][0:SHIFT, h, S - width:S], start=True, stop=True)
                        last.then_inc(ring_full, 1)

                def shifts(g):
                    pe.wait_ge(shift_lo, START + NG * i + g + 1)
                    b = acquire("shift", g)
                    for t in range(NT):
                        last = nc.tensor.transpose(b[:, t * P:(t + 1) * P],
                                                   shift[:, t].rearrange("p h e -> p (h e)").bitcast(F32), ident[:])
                    last.then_inc(ring_full, 1)

                def heads(g, out, left):
                    for t in range(NT):
                        for h in range(GH):
                            last = nc.tensor.matmul(out[h * HD:(h + 1) * HD, t * P:S], left(t, h),
                                                    prob[:, h, KOFF[t]:KOFF[t] + S - t * P],
                                                    start=(t == 0), stop=(t == NT - 1), skip_group_check=True)
                    return last

                def values(g):
                    pe.wait_ge(masked, START + 2 * GH * (NG * i + g + 1))
                    pe.wait_ge(o_ready, START + NG * i + g)
                    heads(g, o_bank, lambda t, h: v[:, t, (GH * g + h) * HD:(GH * g + h + 1) * HD])

                def sums(g):
                    heads(g, sum_bank, lambda t, h: ones[:]).then_inc(pv_done, 1)

                def expert_down(g):
                    pe.wait_ge(heT_ready, START + PAIRS * i + g + 1)
                    pe.wait_ge(dn_in, START + 32 * (PAIRS * i + g + 1))
                    for c in range(IC):
                        for ab in range(2):
                            last = nc.tensor.matmul(eb[ab * CAP:(ab + 1) * CAP, :], heT[:, c, ab * CAP:(ab + 1) * CAP],
                                                    wdn[:, ab, c], start=(c == 0), stop=(c == IC - 1),
                                                    skip_group_check=True)
                    last.then_inc(ye_full, 1)

                def project(t, j):
                    b = acquire("qk", t, j) if j < 2 else acquire("v", t)
                    three_products(nc, b[:], lambda a, k: xo[a][:, k, t * P:(t + 1) * P],
                                   lambda a, k: w_parts[a][:, j, k], range(KC)).then_inc(ring_full, 1)

                def output(t, groups):
                    b = acquire("wo", t) if groups[0] == 0 else bank_of("wo", t)
                    for g in groups:
                        for m, (p, q) in enumerate(((0, 0), (0, 1), (1, 0))):
                            last = nc.tensor.matmul(b[:], xo[p][:, g, t * P:(t + 1) * P], w_parts[q][:, 3, g],
                                                    start=(g == 0 and m == 0), stop=(g == NG - 1 and m == 2))
                    if groups[-1] == NG - 1:
                        last.then_inc(ring_full, 1)

                pe.wait_ge(x_in, START + 16 * (i + 1))
                for k in range(KC):
                    b = acquire("x", k)
                    for t in range(NT):
                        last = nc.tensor.transpose(b[:, t * P:(t + 1) * P], qk[:, 0, t, k * P:(k + 1) * P], ident[:])
                    last.then_inc(ring_full, 1)
                expert_down(0)
                pe.wait_ge(xo_lo, START + KC * (i + 1))
                for t in range(NT):
                    project(t, 0)
                    project(t, 1)
                project(0, 2)
                project(1, 2)
                stack(0)
                for g in range(NG):
                    scores(g, 0)
                    if g:
                        values(g - 1)
                    else:
                        project(2, 2)
                    scores(g, 1)
                    if g:
                        sums(g - 1)
                    else:
                        project(3, 2)
                    scores(g, 2)
                    if g:
                        expert_down(g)
                    next_pair = g + 1 < PAIRS or more
                    if next_pair:
                        expert_rows(i, g + 1)
                    shifts(g)
                    scores_t(g, 0)
                    if next_pair:
                        expert_gate_up(i, g + 1)
                    scores_t(g, 1)
                    if g < NG - 1:
                        stack(g + 1)
                    if next_pair:
                        expert_turn(i, g + 1)
                pe.wait_ge(o_lo, START + NG * (i + 1) - 1)
                output(0, range(NG - 1))
                output(1, range(NG - 1))
                values(NG - 1)
                sums(NG - 1)
                output(2, range(NG - 1))
                output(3, range(NG - 1))
                pe.wait_ge(o_lo, START + NG * (i + 1))
                for t in range(NT):
                    output(t, [NG - 1])

            all_sequences(sequence, pe)


_OUT_ROWS = T + CAP


def _constants():
    p = np.arange(P, dtype=np.float32)
    c = {}
    c["ident"] = np.eye(P, dtype=np.float32)
    c["iota_e"] = np.tile(np.arange(E, dtype=np.float32), (P, 1))
    c["lower"] = (p[:, None] < p[None, :]).astype(np.float32)
    c["tok0"] = p[:, None] + P * np.arange(NT, dtype=np.float32)[None, :]
    c["spill0"] = np.float32(E * CAP) + p[:, None] * (NT * TOPK) + np.arange(NT * TOPK, dtype=np.float32)[None, :]
    slots = np.zeros((E, CAP, 2), np.float32)
    slots[:, :, 0] = T + np.arange(CAP)
    c["slots0"] = slots.reshape(E * CAP, 2)
    c["zeros"] = np.zeros((CAP, H), np.float32)
    inv_freq = 1.0 / 10000.0 ** (np.arange(0, HD, 2, dtype=np.float32) / HD)
    freqs = np.einsum("i,j->ij", np.arange(S, dtype=np.float32), inv_freq)
    emb = np.concatenate((freqs, freqs), axis=-1)
    sign = np.where(np.arange(HD) < HD // 2, np.float32(-1), np.float32(1))
    c["cos"] = np.ascontiguousarray(np.cos(emb).astype(np.float32).reshape(NT, P, HD).transpose(1, 0, 2))
    c["sin"] = np.ascontiguousarray((np.sin(emb).astype(np.float32) * sign).reshape(NT, P, HD).transpose(1, 0, 2))
    mask = np.zeros((P, S), np.float32)
    mask[:, S - P:] = np.where(p[None, :] <= p[:, None], 0.0, -1e30)
    c["mask"] = mask
    return c


def kernel(**inputs):
    import concourse.bacc as _bacc
    from concourse.bass_utils import run_bass_kernel_spmd as _run

    g = {k: np.asarray(v) for k, v in inputs.items()}
    arrays = {
        "x": g["L0_attn_hidden_states"].reshape(T, H),
        "wT": np.stack([g[f"L0_attn_W{n}"].T for n in "qkvo"]),
        "wrT2": np.concatenate([g["L0_ffn_w_router"].T] * 2, axis=1),
        "sh_gate": g["L0_ffn_w_sh_gate"], "sh_up": g["L0_ffn_w_sh_up"], "sh_down": g["L0_ffn_w_sh_down"],
        "w_gate": g["L0_ffn_w_gate"], "w_up": g["L0_ffn_w_up"], "w_down": g["L0_ffn_w_down"],
    }
    arrays.update(_constants())
    arrays = {k: np.ascontiguousarray(v) for k, v in arrays.items()}
    nc = _bacc.Bacc("TRN2", target_bir_lowering=False, num_devices=1,
                    dynamic_dma_scratch_size=8192)
    d = {k: nc.dram_tensor(f"in_{k}", v.shape, mybir.dt.from_np(v.dtype), kind="ExternalInput").ap()
         for k, v in arrays.items()}
    d["out"] = nc.dram_tensor("out_rows", [_OUT_ROWS, H], F32, kind="ExternalOutput").ap()
    d["xn_rows"] = nc.dram_tensor("xn_rows", [T + CAP, H], F32).ap()
    d["slots"] = nc.dram_tensor("slots", [E * CAP + T * TOPK, 2], F32).ap()
    build(nc, d)
    r = _run(nc, [{f"in_{k}": v for k, v in arrays.items()}], core_ids=[0])
    return r.results[0]["out_rows"][0:T].reshape(B, S, H)
```
